# Optimizing a Trainium2 kernel written in Bass

```python
import numpy as np
import jax
import jax.numpy as jnp

def _softmax(x, axis=-1):
    return jax.nn.softmax(x, axis=axis)
def _gelu(x):
    return jax.nn.gelu(x, approximate=True)
def _silu(x):
    return jax.nn.silu(x)
def _sigmoid(x):
    return jax.nn.sigmoid(x)
def _layernorm(x, axis=-1, eps=1e-5):
    m = jnp.mean(x, axis=axis, keepdims=True)
    v = jnp.var(x, axis=axis, keepdims=True)
    return (x - m) / jnp.sqrt(v + eps)
def _scatter_add(tgt, idx, src, axis=0):
    return tgt.at[idx].add(src)
def _segment_sum(src, seg, n):
    return jax.ops.segment_sum(src, seg, n)

kernel_name = 'mk_rec_standalone_d1_rec_a0e353'

def setup_inputs(seed: int = 0):
    np.random.seed(seed)
    _w = jnp.asarray
    def _rec_inputs():
        import jax
        import jax.numpy as jnp
        _rk = jax.random.key(seed)
        r_seq = jnp.stack([jax.random.randint(jax.random.fold_in(jax.random.fold_in(_rk, 1), 0), (1024,), 171, 99919, jnp.int32), jax.random.randint(jax.random.fold_in(jax.random.fold_in(_rk, 1), 1), (1024,), 77, 99188, jnp.int32), jax.random.randint(jax.random.fold_in(jax.random.fold_in(_rk, 1), 2), (1024,), 29, 99986, jnp.int32), jax.random.randint(jax.random.fold_in(jax.random.fold_in(_rk, 1), 3), (1024,), 67, 99858, jnp.int32), jax.random.randint(jax.random.fold_in(jax.random.fold_in(_rk, 1), 4), (1024,), 68, 99700, jnp.int32), jax.random.randint(jax.random.fold_in(jax.random.fold_in(_rk, 1), 5), (1024,), 167, 99906, jnp.int32), jax.random.randint(jax.random.fold_in(jax.random.fold_in(_rk, 1), 6), (1024,), 161, 99745, jnp.int32), jax.random.randint(jax.random.fold_in(jax.random.fold_in(_rk, 1), 7), (1024,), 113, 99925, jnp.int32), jax.random.randint(jax.random.fold_in(jax.random.fold_in(_rk, 1), 8), (1024,), 114, 99400, jnp.int32), jax.random.randint(jax.random.fold_in(jax.random.fold_in(_rk, 1), 9), (1024,), 13, 99632, jnp.int32), jax.random.randint(jax.random.fold_in(jax.random.fold_in(_rk, 1), 10), (1024,), 387, 99701, jnp.int32), jax.random.randint(jax.random.fold_in(jax.random.fold_in(_rk, 1), 11), (1024,), 146, 99448, jnp.int32), jax.random.randint(jax.random.fold_in(jax.random.fold_in(_rk, 1), 12), (1024,), 80, 99736, jnp.int32), jax.random.randint(jax.random.fold_in(jax.random.fold_in(_rk, 1), 13), (1024,), 455, 99555, jnp.int32), jax.random.randint(jax.random.fold_in(jax.random.fold_in(_rk, 1), 14), (1024,), 182, 99892, jnp.int32), jax.random.randint(jax.random.fold_in(jax.random.fold_in(_rk, 1), 15), (1024,), 159, 99939, jnp.int32), jax.random.randint(jax.random.fold_in(jax.random.fold_in(_rk, 1), 16), (1024,), 28, 99865, jnp.int32), jax.random.randint(jax.random.fold_in(jax.random.fold_in(_rk, 1), 17), (1024,), 90, 99935, jnp.int32), jax.random.randint(jax.random.fold_in(jax.random.fold_in(_rk, 1), 18), (1024,), 86, 99796, jnp.int32), jax.random.randint(jax.random.fold_in(jax.random.fold_in(_rk, 1), 19), (1024,), 18, 99904, jnp.int32), jax.random.randint(jax.random.fold_in(jax.random.fold_in(_rk, 1), 20), (1024,), 78, 99909, jnp.int32), jax.random.randint(jax.random.fold_in(jax.random.fold_in(_rk, 1), 21), (1024,), 131, 99946, jnp.int32), jax.random.randint(jax.random.fold_in(jax.random.fold_in(_rk, 1), 22), (1024,), 264, 99913, jnp.int32), jax.random.randint(jax.random.fold_in(jax.random.fold_in(_rk, 1), 23), (1024,), 203, 99844, jnp.int32), jax.random.randint(jax.random.fold_in(jax.random.fold_in(_rk, 1), 24), (1024,), 126, 99953, jnp.int32), jax.random.randint(jax.random.fold_in(jax.random.fold_in(_rk, 1), 25), (1024,), 90, 99942, jnp.int32), jax.random.randint(jax.random.fold_in(jax.random.fold_in(_rk, 1), 26), (1024,), 163, 99823, jnp.int32), jax.random.randint(jax.random.fold_in(jax.random.fold_in(_rk, 1), 27), (1024,), 104, 99938, jnp.int32), jax.random.randint(jax.random.fold_in(jax.random.fold_in(_rk, 1), 28), (1024,), 138, 99972, jnp.int32), jax.random.randint(jax.random.fold_in(jax.random.fold_in(_rk, 1), 29), (1024,), 190, 99946, jnp.int32), jax.random.randint(jax.random.fold_in(jax.random.fold_in(_rk, 1), 30), (1024,), 394, 99874, jnp.int32), jax.random.randint(jax.random.fold_in(jax.random.fold_in(_rk, 1), 31), (1024,), 192, 99871, jnp.int32), jax.random.randint(jax.random.fold_in(jax.random.fold_in(_rk, 1), 32), (1024,), 100, 99909, jnp.int32), jax.random.randint(jax.random.fold_in(jax.random.fold_in(_rk, 1), 33), (1024,), 47, 99778, jnp.int32), jax.random.randint(jax.random.fold_in(jax.random.fold_in(_rk, 1), 34), (1024,), 262, 99945, jnp.int32), jax.random.randint(jax.random.fold_in(jax.random.fold_in(_rk, 1), 35), (1024,), 60, 99998, jnp.int32), jax.random.randint(jax.random.fold_in(jax.random.fold_in(_rk, 1), 36), (1024,), 302, 99923, jnp.int32), jax.random.randint(jax.random.fold_in(jax.random.fold_in(_rk, 1), 37), (1024,), 54, 99906, jnp.int32), jax.random.randint(jax.random.fold_in(jax.random.fold_in(_rk, 1), 38), (1024,), 144, 99955, jnp.int32), jax.random.randint(jax.random.fold_in(jax.random.fold_in(_rk, 1), 39), (1024,), 14, 99839, jnp.int32), jax.random.randint(jax.random.fold_in(jax.random.fold_in(_rk, 1), 40), (1024,), 171, 99738, jnp.int32), jax.random.randint(jax.random.fold_in(jax.random.fold_in(_rk, 1), 41), (1024,), 33, 99712, jnp.int32), jax.random.randint(jax.random.fold_in(jax.random.fold_in(_rk, 1), 42), (1024,), 51, 99990, jnp.int32), jax.random.randint(jax.random.fold_in(jax.random.fold_in(_rk, 1), 43), (1024,), 45, 99982, jnp.int32), jax.random.randint(jax.random.fold_in(jax.random.fold_in(_rk, 1), 44), (1024,), 86, 99940, jnp.int32), jax.random.randint(jax.random.fold_in(jax.random.fold_in(_rk, 1), 45), (1024,), 263, 99699, jnp.int32), jax.random.randint(jax.random.fold_in(jax.random.fold_in(_rk, 1), 46), (1024,), 300, 99582, jnp.int32), jax.random.randint(jax.random.fold_in(jax.random.fold_in(_rk, 1), 47), (1024,), 95, 99952, jnp.int32), jax.random.randint(jax.random.fold_in(jax.random.fold_in(_rk, 1), 48), (1024,), 156, 99964, jnp.int32), jax.random.randint(jax.random.fold_in(jax.random.fold_in(_rk, 1), 49), (1024,), 145, 99578, jnp.int32), jax.random.randint(jax.random.fold_in(jax.random.fold_in(_rk, 1), 50), (1024,), 433, 99602, jnp.int32), jax.random.randint(jax.random.fold_in(jax.random.fold_in(_rk, 1), 51), (1024,), 252, 99952, jnp.int32), jax.random.randint(jax.random.fold_in(jax.random.fold_in(_rk, 1), 52), (1024,), 281, 99727, jnp.int32), jax.random.randint(jax.random.fold_in(jax.random.fold_in(_rk, 1), 53), (1024,), 347, 99808, jnp.int32), jax.random.randint(jax.random.fold_in(jax.random.fold_in(_rk, 1), 54), (1024,), 875, 99948, jnp.int32), jax.random.randint(jax.random.fold_in(jax.random.fold_in(_rk, 1), 55), (1024,), 83, 99942, jnp.int32), jax.random.randint(jax.random.fold_in(jax.random.fold_in(_rk, 1), 56), (1024,), 1, 99971, jnp.int32), jax.random.randint(jax.random.fold_in(jax.random.fold_in(_rk, 1), 57), (1024,), 31, 99986, jnp.int32), jax.random.randint(jax.random.fold_in(jax.random.fold_in(_rk, 1), 58), (1024,), 128, 99996, jnp.int32), jax.random.randint(jax.random.fold_in(jax.random.fold_in(_rk, 1), 59), (1024,), 72, 99817, jnp.int32), jax.random.randint(jax.random.fold_in(jax.random.fold_in(_rk, 1), 60), (1024,), 127, 99745, jnp.int32), jax.random.randint(jax.random.fold_in(jax.random.fold_in(_rk, 1), 61), (1024,), 181, 99797, jnp.int32), jax.random.randint(jax.random.fold_in(jax.random.fold_in(_rk, 1), 62), (1024,), 231, 99840, jnp.int32), jax.random.randint(jax.random.fold_in(jax.random.fold_in(_rk, 1), 63), (1024,), 96, 99973, jnp.int32), jax.random.randint(jax.random.fold_in(jax.random.fold_in(_rk, 1), 64), (1024,), 51, 99950, jnp.int32), jax.random.randint(jax.random.fold_in(jax.random.fold_in(_rk, 1), 65), (1024,), 42, 99755, jnp.int32), jax.random.randint(jax.random.fold_in(jax.random.fold_in(_rk, 1), 66), (1024,), 553, 99291, jnp.int32), jax.random.randint(jax.random.fold_in(jax.random.fold_in(_rk, 1), 67), (1024,), 20, 99962, jnp.int32), jax.random.randint(jax.random.fold_in(jax.random.fold_in(_rk, 1), 68), (1024,), 11, 99506, jnp.int32), jax.random.randint(jax.random.fold_in(jax.random.fold_in(_rk, 1), 69), (1024,), 121, 99714, jnp.int32), jax.random.randint(jax.random.fold_in(jax.random.fold_in(_rk, 1), 70), (1024,), 250, 99746, jnp.int32), jax.random.randint(jax.random.fold_in(jax.random.fold_in(_rk, 1), 71), (1024,), 325, 99862, jnp.int32), jax.random.randint(jax.random.fold_in(jax.random.fold_in(_rk, 1), 72), (1024,), 129, 99466, jnp.int32), jax.random.randint(jax.random.fold_in(jax.random.fold_in(_rk, 1), 73), (1024,), 372, 99861, jnp.int32), jax.random.randint(jax.random.fold_in(jax.random.fold_in(_rk, 1), 74), (1024,), 5, 99896, jnp.int32), jax.random.randint(jax.random.fold_in(jax.random.fold_in(_rk, 1), 75), (1024,), 193, 99672, jnp.int32), jax.random.randint(jax.random.fold_in(jax.random.fold_in(_rk, 1), 76), (1024,), 492, 99911, jnp.int32), jax.random.randint(jax.random.fold_in(jax.random.fold_in(_rk, 1), 77), (1024,), 15, 99856, jnp.int32), jax.random.randint(jax.random.fold_in(jax.random.fold_in(_rk, 1), 78), (1024,), 44, 99993, jnp.int32), jax.random.randint(jax.random.fold_in(jax.random.fold_in(_rk, 1), 79), (1024,), 53, 99881, jnp.int32), jax.random.randint(jax.random.fold_in(jax.random.fold_in(_rk, 1), 80), (1024,), 786, 99754, jnp.int32), jax.random.randint(jax.random.fold_in(jax.random.fold_in(_rk, 1), 81), (1024,), 116, 99810, jnp.int32), jax.random.randint(jax.random.fold_in(jax.random.fold_in(_rk, 1), 82), (1024,), 212, 99535, jnp.int32), jax.random.randint(jax.random.fold_in(jax.random.fold_in(_rk, 1), 83), (1024,), 325, 99866, jnp.int32), jax.random.randint(jax.random.fold_in(jax.random.fold_in(_rk, 1), 84), (1024,), 171, 99660, jnp.int32), jax.random.randint(jax.random.fold_in(jax.random.fold_in(_rk, 1), 85), (1024,), 19, 99949, jnp.int32), jax.random.randint(jax.random.fold_in(jax.random.fold_in(_rk, 1), 86), (1024,), 148, 99807, jnp.int32), jax.random.randint(jax.random.fold_in(jax.random.fold_in(_rk, 1), 87), (1024,), 68, 99893, jnp.int32), jax.random.randint(jax.random.fold_in(jax.random.fold_in(_rk, 1), 88), (1024,), 53, 99881, jnp.int32), jax.random.randint(jax.random.fold_in(jax.random.fold_in(_rk, 1), 89), (1024,), 921, 99531, jnp.int32), jax.random.randint(jax.random.fold_in(jax.random.fold_in(_rk, 1), 90), (1024,), 276, 99937, jnp.int32), jax.random.randint(jax.random.fold_in(jax.random.fold_in(_rk, 1), 91), (1024,), 1, 99514, jnp.int32), jax.random.randint(jax.random.fold_in(jax.random.fold_in(_rk, 1), 92), (1024,), 103, 99847, jnp.int32), jax.random.randint(jax.random.fold_in(jax.random.fold_in(_rk, 1), 93), (1024,), 329, 99980, jnp.int32), jax.random.randint(jax.random.fold_in(jax.random.fold_in(_rk, 1), 94), (1024,), 185, 99967, jnp.int32), jax.random.randint(jax.random.fold_in(jax.random.fold_in(_rk, 1), 95), (1024,), 294, 99626, jnp.int32), jax.random.randint(jax.random.fold_in(jax.random.fold_in(_rk, 1), 96), (1024,), 215, 99847, jnp.int32), jax.random.randint(jax.random.fold_in(jax.random.fold_in(_rk, 1), 97), (1024,), 11, 99516, jnp.int32), jax.random.randint(jax.random.fold_in(jax.random.fold_in(_rk, 1), 98), (1024,), 671, 99952, jnp.int32), jax.random.randint(jax.random.fold_in(jax.random.fold_in(_rk, 1), 99), (1024,), 178, 99919, jnp.int32), jax.random.randint(jax.random.fold_in(jax.random.fold_in(_rk, 1), 100), (1024,), 76, 99975, jnp.int32), jax.random.randint(jax.random.fold_in(jax.random.fold_in(_rk, 1), 101), (1024,), 55, 99501, jnp.int32), jax.random.randint(jax.random.fold_in(jax.random.fold_in(_rk, 1), 102), (1024,), 92, 99778, jnp.int32), jax.random.randint(jax.random.fold_in(jax.random.fold_in(_rk, 1), 103), (1024,), 417, 99987, jnp.int32), jax.random.randint(jax.random.fold_in(jax.random.fold_in(_rk, 1), 104), (1024,), 28, 99965, jnp.int32), jax.random.randint(jax.random.fold_in(jax.random.fold_in(_rk, 1), 105), (1024,), 36, 99663, jnp.int32), jax.random.randint(jax.random.fold_in(jax.random.fold_in(_rk, 1), 106), (1024,), 624, 99965, jnp.int32), jax.random.randint(jax.random.fold_in(jax.random.fold_in(_rk, 1), 107), (1024,), 45, 99945, jnp.int32), jax.random.randint(jax.random.fold_in(jax.random.fold_in(_rk, 1), 108), (1024,), 36, 99951, jnp.int32), jax.random.randint(jax.random.fold_in(jax.random.fold_in(_rk, 1), 109), (1024,), 15, 99854, jnp.int32), jax.random.randint(jax.random.fold_in(jax.random.fold_in(_rk, 1), 110), (1024,), 39, 99839, jnp.int32), jax.random.randint(jax.random.fold_in(jax.random.fold_in(_rk, 1), 111), (1024,), 409, 99964, jnp.int32), jax.random.randint(jax.random.fold_in(jax.random.fold_in(_rk, 1), 112), (1024,), 39, 99990, jnp.int32), jax.random.randint(jax.random.fold_in(jax.random.fold_in(_rk, 1), 113), (1024,), 467, 99821, jnp.int32), jax.random.randint(jax.random.fold_in(jax.random.fold_in(_rk, 1), 114), (1024,), 364, 99626, jnp.int32), jax.random.randint(jax.random.fold_in(jax.random.fold_in(_rk, 1), 115), (1024,), 207, 99917, jnp.int32), jax.random.randint(jax.random.fold_in(jax.random.fold_in(_rk, 1), 116), (1024,), 259, 99729, jnp.int32), jax.random.randint(jax.random.fold_in(jax.random.fold_in(_rk, 1), 117), (1024,), 28, 99988, jnp.int32), jax.random.randint(jax.random.fold_in(jax.random.fold_in(_rk, 1), 118), (1024,), 7, 99909, jnp.int32), jax.random.randint(jax.random.fold_in(jax.random.fold_in(_rk, 1), 119), (1024,), 159, 99904, jnp.int32), jax.random.randint(jax.random.fold_in(jax.random.fold_in(_rk, 1), 120), (1024,), 17, 99900, jnp.int32), jax.random.randint(jax.random.fold_in(jax.random.fold_in(_rk, 1), 121), (1024,), 231, 99987, jnp.int32), jax.random.randint(jax.random.fold_in(jax.random.fold_in(_rk, 1), 122), (1024,), 282, 99501, jnp.int32), jax.random.randint(jax.random.fold_in(jax.random.fold_in(_rk, 1), 123), (1024,), 32, 99652, jnp.int32), jax.random.randint(jax.random.fold_in(jax.random.fold_in(_rk, 1), 124), (1024,), 78, 99494, jnp.int32), jax.random.randint(jax.random.fold_in(jax.random.fold_in(_rk, 1), 125), (1024,), 418, 99629, jnp.int32), jax.random.randint(jax.random.fold_in(jax.random.fold_in(_rk, 1), 126), (1024,), 98, 99843, jnp.int32), jax.random.randint(jax.random.fold_in(jax.random.fold_in(_rk, 1), 127), (1024,), 350, 99447, jnp.int32), jax.random.randint(jax.random.fold_in(jax.random.fold_in(_rk, 1), 128), (1024,), 42, 99778, jnp.int32), jax.random.randint(jax.random.fold_in(jax.random.fold_in(_rk, 1), 129), (1024,), 431, 99743, jnp.int32), jax.random.randint(jax.random.fold_in(jax.random.fold_in(_rk, 1), 130), (1024,), 118, 99903, jnp.int32), jax.random.randint(jax.random.fold_in(jax.random.fold_in(_rk, 1), 131), (1024,), 194, 99794, jnp.int32), jax.random.randint(jax.random.fold_in(jax.random.fold_in(_rk, 1), 132), (1024,), 22, 99954, jnp.int32), jax.random.randint(jax.random.fold_in(jax.random.fold_in(_rk, 1), 133), (1024,), 17, 99770, jnp.int32), jax.random.randint(jax.random.fold_in(jax.random.fold_in(_rk, 1), 134), (1024,), 46, 99855, jnp.int32), jax.random.randint(jax.random.fold_in(jax.random.fold_in(_rk, 1), 135), (1024,), 804, 99713, jnp.int32), jax.random.randint(jax.random.fold_in(jax.random.fold_in(_rk, 1), 136), (1024,), 593, 99653, jnp.int32), jax.random.randint(jax.random.fold_in(jax.random.fold_in(_rk, 1), 137), (1024,), 123, 99896, jnp.int32), jax.random.randint(jax.random.fold_in(jax.random.fold_in(_rk, 1), 138), (1024,), 193, 99684, jnp.int32), jax.random.randint(jax.random.fold_in(jax.random.fold_in(_rk, 1), 139), (1024,), 655, 99978, jnp.int32), jax.random.randint(jax.random.fold_in(jax.random.fold_in(_rk, 1), 140), (1024,), 405, 99969, jnp.int32), jax.random.randint(jax.random.fold_in(jax.random.fold_in(_rk, 1), 141), (1024,), 92, 99884, jnp.int32), jax.random.randint(jax.random.fold_in(jax.random.fold_in(_rk, 1), 142), (1024,), 169, 99691, jnp.int32), jax.random.randint(jax.random.fold_in(jax.random.fold_in(_rk, 1), 143), (1024,), 396, 99896, jnp.int32), jax.random.randint(jax.random.fold_in(jax.random.fold_in(_rk, 1), 144), (1024,), 5, 99706, jnp.int32), jax.random.randint(jax.random.fold_in(jax.random.fold_in(_rk, 1), 145), (1024,), 270, 99879, jnp.int32), jax.random.randint(jax.random.fold_in(jax.random.fold_in(_rk, 1), 146), (1024,), 142, 99894, jnp.int32), jax.random.randint(jax.random.fold_in(jax.random.fold_in(_rk, 1), 147), (1024,), 62, 99921, jnp.int32), jax.random.randint(jax.random.fold_in(jax.random.fold_in(_rk, 1), 148), (1024,), 3, 99767, jnp.int32), jax.random.randint(jax.random.fold_in(jax.random.fold_in(_rk, 1), 149), (1024,), 162, 99523, jnp.int32), jax.random.randint(jax.random.fold_in(jax.random.fold_in(_rk, 1), 150), (1024,), 158, 99917, jnp.int32), jax.random.randint(jax.random.fold_in(jax.random.fold_in(_rk, 1), 151), (1024,), 276, 99790, jnp.int32), jax.random.randint(jax.random.fold_in(jax.random.fold_in(_rk, 1), 152), (1024,), 168, 99818, jnp.int32), jax.random.randint(jax.random.fold_in(jax.random.fold_in(_rk, 1), 153), (1024,), 862, 99057, jnp.int32), jax.random.randint(jax.random.fold_in(jax.random.fold_in(_rk, 1), 154), (1024,), 226, 99887, jnp.int32), jax.random.randint(jax.random.fold_in(jax.random.fold_in(_rk, 1), 155), (1024,), 176, 99988, jnp.int32), jax.random.randint(jax.random.fold_in(jax.random.fold_in(_rk, 1), 156), (1024,), 153, 99832, jnp.int32), jax.random.randint(jax.random.fold_in(jax.random.fold_in(_rk, 1), 157), (1024,), 208, 99870, jnp.int32), jax.random.randint(jax.random.fold_in(jax.random.fold_in(_rk, 1), 158), (1024,), 95, 99483, jnp.int32), jax.random.randint(jax.random.fold_in(jax.random.fold_in(_rk, 1), 159), (1024,), 180, 99856, jnp.int32), jax.random.randint(jax.random.fold_in(jax.random.fold_in(_rk, 1), 160), (1024,), 603, 99904, jnp.int32), jax.random.randint(jax.random.fold_in(jax.random.fold_in(_rk, 1), 161), (1024,), 231, 99784, jnp.int32), jax.random.randint(jax.random.fold_in(jax.random.fold_in(_rk, 1), 162), (1024,), 28, 99632, jnp.int32), jax.random.randint(jax.random.fold_in(jax.random.fold_in(_rk, 1), 163), (1024,), 6, 99860, jnp.int32), jax.random.randint(jax.random.fold_in(jax.random.fold_in(_rk, 1), 164), (1024,), 15, 99886, jnp.int32), jax.random.randint(jax.random.fold_in(jax.random.fold_in(_rk, 1), 165), (1024,), 131, 99907, jnp.int32), jax.random.randint(jax.random.fold_in(jax.random.fold_in(_rk, 1), 166), (1024,), 400, 99988, jnp.int32), jax.random.randint(jax.random.fold_in(jax.random.fold_in(_rk, 1), 167), (1024,), 10, 99687, jnp.int32), jax.random.randint(jax.random.fold_in(jax.random.fold_in(_rk, 1), 168), (1024,), 58, 99998, jnp.int32), jax.random.randint(jax.random.fold_in(jax.random.fold_in(_rk, 1), 169), (1024,), 260, 99957, jnp.int32), jax.random.randint(jax.random.fold_in(jax.random.fold_in(_rk, 1), 170), (1024,), 81, 99987, jnp.int32), jax.random.randint(jax.random.fold_in(jax.random.fold_in(_rk, 1), 171), (1024,), 163, 99770, jnp.int32), jax.random.randint(jax.random.fold_in(jax.random.fold_in(_rk, 1), 172), (1024,), 122, 99962, jnp.int32), jax.random.randint(jax.random.fold_in(jax.random.fold_in(_rk, 1), 173), (1024,), 64, 99883, jnp.int32), jax.random.randint(jax.random.fold_in(jax.random.fold_in(_rk, 1), 174), (1024,), 275, 99877, jnp.int32), jax.random.randint(jax.random.fold_in(jax.random.fold_in(_rk, 1), 175), (1024,), 10, 99705, jnp.int32), jax.random.randint(jax.random.fold_in(jax.random.fold_in(_rk, 1), 176), (1024,), 262, 99986, jnp.int32), jax.random.randint(jax.random.fold_in(jax.random.fold_in(_rk, 1), 177), (1024,), 164, 99805, jnp.int32), jax.random.randint(jax.random.fold_in(jax.random.fold_in(_rk, 1), 178), (1024,), 277, 99725, jnp.int32), jax.random.randint(jax.random.fold_in(jax.random.fold_in(_rk, 1), 179), (1024,), 185, 99473, jnp.int32), jax.random.randint(jax.random.fold_in(jax.random.fold_in(_rk, 1), 180), (1024,), 35, 99962, jnp.int32), jax.random.randint(jax.random.fold_in(jax.random.fold_in(_rk, 1), 181), (1024,), 282, 99963, jnp.int32), jax.random.randint(jax.random.fold_in(jax.random.fold_in(_rk, 1), 182), (1024,), 225, 99926, jnp.int32), jax.random.randint(jax.random.fold_in(jax.random.fold_in(_rk, 1), 183), (1024,), 65, 99946, jnp.int32), jax.random.randint(jax.random.fold_in(jax.random.fold_in(_rk, 1), 184), (1024,), 119, 99892, jnp.int32), jax.random.randint(jax.random.fold_in(jax.random.fold_in(_rk, 1), 185), (1024,), 177, 99866, jnp.int32), jax.random.randint(jax.random.fold_in(jax.random.fold_in(_rk, 1), 186), (1024,), 24, 99790, jnp.int32), jax.random.randint(jax.random.fold_in(jax.random.fold_in(_rk, 1), 187), (1024,), 131, 99684, jnp.int32), jax.random.randint(jax.random.fold_in(jax.random.fold_in(_rk, 1), 188), (1024,), 114, 99613, jnp.int32), jax.random.randint(jax.random.fold_in(jax.random.fold_in(_rk, 1), 189), (1024,), 180, 99991, jnp.int32), jax.random.randint(jax.random.fold_in(jax.random.fold_in(_rk, 1), 190), (1024,), 88, 99788, jnp.int32), jax.random.randint(jax.random.fold_in(jax.random.fold_in(_rk, 1), 191), (1024,), 14, 99896, jnp.int32), jax.random.randint(jax.random.fold_in(jax.random.fold_in(_rk, 1), 192), (1024,), 79, 99768, jnp.int32), jax.random.randint(jax.random.fold_in(jax.random.fold_in(_rk, 1), 193), (1024,), 229, 99942, jnp.int32), jax.random.randint(jax.random.fold_in(jax.random.fold_in(_rk, 1), 194), (1024,), 52, 99879, jnp.int32), jax.random.randint(jax.random.fold_in(jax.random.fold_in(_rk, 1), 195), (1024,), 61, 99977, jnp.int32), jax.random.randint(jax.random.fold_in(jax.random.fold_in(_rk, 1), 196), (1024,), 476, 99809, jnp.int32), jax.random.randint(jax.random.fold_in(jax.random.fold_in(_rk, 1), 197), (1024,), 91, 99425, jnp.int32), jax.random.randint(jax.random.fold_in(jax.random.fold_in(_rk, 1), 198), (1024,), 252, 99792, jnp.int32), jax.random.randint(jax.random.fold_in(jax.random.fold_in(_rk, 1), 199), (1024,), 49, 99873, jnp.int32)], axis=1)
        return r_seq
    r_seq = _rec_inputs()
    def _L0_rec_setup():
        import jax, jax.numpy as jnp
        import numpy as np
        N_ITEMS = 100000
        HIDDEN = 128
        SEQ = 200
        K = 4
        ITERS = 3
        POW = 1.0
        BATCH = 512

        def squash(s):
            n = jnp.linalg.norm(s, axis=-1, keepdims=True)
            n2 = n * n
            return n2 / (1.0 + n2) * (s / (n + 1e-12))
        key = jax.random.key(seed)
        k1, k2, k3, k4 = jax.random.split(key, 4)
        seq = jax.random.randint(k1, (BATCH, SEQ), 0, N_ITEMS)
        emb_table = jax.random.normal(k2, (N_ITEMS, HIDDEN), dtype=jnp.float32) * 0.02
        emb_table = emb_table.at[0].set(0.0)
        bound = 1.0 / np.sqrt(HIDDEN)
        s_w = jax.random.uniform(k3, (HIDDEN, HIDDEN * K), dtype=jnp.float32, minval=-bound, maxval=bound)
        s_b = jax.random.uniform(k4, (HIDDEN * K,), dtype=jnp.float32, minval=-bound, maxval=bound)
        return {'seq': seq, 'emb_table': emb_table, 's_w': s_w, 's_b': s_b}
    _L0_rec_all = _L0_rec_setup()
    _L0_rec_in = {k: v for k, v in _L0_rec_all.items() if k in ('emb_table', 's_w', 's_b', )}
    del _L0_rec_all

    return {
        "r_seq": r_seq,
        "L0_rec_emb_table": _L0_rec_in["emb_table"],
        "L0_rec_s_w": _L0_rec_in["s_w"],
        "L0_rec_s_b": _L0_rec_in["s_b"],
    }

def reference(r_seq, L0_rec_emb_table, L0_rec_s_w, L0_rec_s_b):
    import jax
    import jax.numpy as jnp
    def _L0_rec_ref(seq, emb_table, s_w, s_b):
        import jax, jax.numpy as jnp
        import numpy as np
        N_ITEMS = 100000
        HIDDEN = 128
        SEQ = 200
        K = 4
        ITERS = 3
        POW = 1.0
        BATCH = 512

        def squash(s):
            n = jnp.linalg.norm(s, axis=-1, keepdims=True)
            n2 = n * n
            return n2 / (1.0 + n2) * (s / (n + 1e-12))
        mask = (seq != 0).astype(jnp.float32)
        lut = emb_table.at[0].set(jax.lax.stop_gradient(emb_table[0]))
        item_emb = lut[seq]
        u = item_emb @ s_w + s_b
        b, s = seq.shape
        u = u.reshape(b, s, K, HIDDEN).transpose(0, 2, 1, 3)
        u = jax.lax.stop_gradient(u)
        m = mask[:, None, :]
        capsule_b = jnp.zeros((b, K, s), dtype=jnp.float32)
        v = None
        for _ in range(ITERS):
            capsule_b = jnp.where(m == 0, -10000.0, capsule_b)
            c = jax.nn.softmax(capsule_b, axis=1)
            sv = jnp.einsum('bks,bksd->bkd', c, u)
            v = squash(sv)
            capsule_b = capsule_b + jnp.einsum('bksd,bkd->bks', u, v)
        interest = v
        last_item = lut[seq[:, -1]]
        att = jnp.einsum('bd,bkd->bk', last_item, interest)
        att = att ** POW
        w = jax.nn.softmax(att, axis=-1)
        final = jnp.einsum('bk,bkd->bd', w, interest)
        score = final @ emb_table.T
        return score

    y = _L0_rec_ref(r_seq, L0_rec_emb_table, L0_rec_s_w, L0_rec_s_b)
    return y


_drawn_inputs = setup_inputs


def setup_inputs(seed=0):
    import zlib

    import numpy as np

    out = dict(_drawn_inputs(seed))
    spreads = {}
    factors = {'L0_rec_s_w': 3.263}
    for name, (base, spread) in spreads.items():
        noise = np.random.default_rng([zlib.crc32(name.encode()), seed]).standard_normal(out[name].shape)
        drawn = base * np.exp(spread * noise) if base else spread * noise
        out[name] = jnp.asarray(drawn.astype(out[name].dtype))
    for name, factor in factors.items():
        out[name] = (out[name] * factor).astype(out[name].dtype)
    return out
```

```python
from contextlib import ExitStack

import numpy as np

import concourse.bass as bass
from concourse import mybir

F32 = mybir.dt.float32
BF16 = mybir.dt.bfloat16
I32 = mybir.dt.int32
U32 = mybir.dt.uint32
ALU = mybir.AluOpType
ACT = mybir.ActivationFunctionType
AX = mybir.AxisListType

P = 128
BATCH, SEQ, K, HID, ITEMS = 1024, 200, 4, 128, 100000
GROUP = 16
TILES = GROUP * SEQ // P
NG = BATCH // GROUP
PADT = TILES + 1
HALF = PADT // 2
PADG = GROUP + 1
SLOTS = 2
PARTS = 3
CHUNK = 5
CHUNKS = TILES // CHUNK
GK = GROUP * K
LW = PARTS * SLOTS * K
RSQRT_MAGIC = 1597463007.0
PIECE = 2500
COLS = 500
NP = ITEMS // PIECE
MT = BATCH // P
NC = PIECE // COLS
RING = 4

FIRST_SEQ = [P * t // SEQ for t in range(TILES)]


def upper(ap):
    names = " ".join("abcd"[: len(ap.shape) - 2])
    v = ap.bitcast(BF16)
    return v.rearrange(f"p {names} (n two) -> p {names} n two", two=2)[..., 1]


def build(nc, index, table, table_t, w, w_t, bias, ident, slot_mask, out):
    ctx = ExitStack()
    with ctx:
        def sb(name, shape, dt=F32):
            return ctx.enter_context(nc.sbuf_tensor(name, shape, dt))

        def ps(name, shape, dt=F32):
            return ctx.enter_context(nc.psum_tensor(name, shape, dt))

        def sem(name):
            return ctx.enter_context(nc.semaphore(name))

        idx = [sb(f"idx{h}", [P, TILES], U32) for h in range(2)]
        emb = [sb(f"emb{h}", [P, TILES, HID]) for h in range(2)]
        rest = [sb(f"rest{h}", [P, TILES, HID]) for h in range(2)]
        low = [sb(f"low{h}", [P, TILES, HID], BF16) for h in range(2)]
        emb_t = [sb(f"emb_t{h}", [P, PARTS, TILES * P], BF16) for h in range(2)]
        mask = [sb(f"mask{h}", [P, PADT, SLOTS, K]) for h in range(2)]
        w_sb = sb("w_sb", [P, 3, K, HID])
        wt_sb = sb("wt_sb", [P, 3, K, HID])
        bias_sb = sb("bias_sb", [P, K])
        bias_n = sb("bias_n", [P, K])
        ident_f = sb("ident_f", [P, P])
        ident_b = sb("ident_b", [P, P], BF16)
        ones_b = sb("ones_b", [P, P], BF16)
        ones_f = sb("ones_f", [P, P])
        zeros_b = sb("zeros_b", [P, 2 * PARTS * PADG * K], BF16)
        slot_sb = sb("slot_sb", [P, PADT, SLOTS, K])
        quarter = sb("quarter", [P, PADT, SLOTS], BF16)
        nonzero = sb("nonzero", [P, PADT])
        pooled = sb("pooled", [P, PARTS + 1, GK])
        count_b = sb("count_b", [P, GROUP, K])
        s_sb = sb("s_sb", [P, GROUP, K])
        sq = sb("sq", [P, GK])
        n2 = sb("n2", [P, GK])
        guess = sb("guess", [P, GK], I32)
        ta, tb, tc, td = (sb(n, [P, GK]) for n in ("ta", "tb", "tc", "td"))
        v_sb = sb("v_sb", [P, PARTS, GROUP, K])
        qb = sb("qb", [P, PARTS, 2, PADG * K])
        summed = sb("summed", [P, PADT, SLOTS, K])
        masked = sb("masked", [P, PADT, SLOTS, K])
        logit = sb("logit", [P, PADT, K])
        delta = sb("delta", [P, PADT, K])
        top = sb("top", [P, PADT])
        less = sb("less", [P, PADT, K])
        ex = sb("ex", [P, PADT, K])
        total = sb("total", [P, PADT])
        inv = sb("inv", [P, PADT])
        prob = sb("prob", [P, PADT, K])
        c_sb = sb("c_sb", [P, PARTS, PADT, SLOTS * K])
        last_t = sb("last_t", [P, GROUP])
        final_t = sb("final_t", [P, BATCH])
        tab = [sb(f"tab{h}", [P, PIECE]) for h in range(2)]
        score = [sb(f"score{r}", [P, PIECE]) for r in range(RING)]

        et_ps = [ps(f"et_ps{i}", [P, 2 * 512], BF16) for i in range(2)]
        l_ps = ps("l_ps", [P, 2, 512])
        p_ps = ps("p_ps", [P, 512])
        m_ps = ps("m_ps", [P, 512])
        sc_ps = [ps(f"sc_ps{i}", [P, 512]) for i in range(2)]
        s_out = m_ps[:, 0:192].rearrange("p (k a b) -> p k a b", k=K, a=PARTS)
        q_out = m_ps[:, 192:384].rearrange("p (k a b) -> p k a b", k=K, a=PARTS)
        n_out = m_ps[:, 384:384 + GK]

        loaded = sem("loaded")
        idx_in = [sem(f"idx_in{h}") for h in range(2)]
        gathered = [[sem(f"gathered{h}_{c}") for c in range(CHUNKS)] for h in range(2)]
        consts_done = sem("consts_done")
        nz_done = sem("nz_done")
        split_done = sem("split_done")
        et_full = sem("et_full")
        et_copied = sem("et_copied")
        p_done = sem("p_done")
        s_done = sem("s_done")
        n_done = sem("n_done")
        q_done = sem("q_done")
        l_done = sem("l_done")
        pooled_ready = sem("pooled_ready")
        sq_ready = sem("sq_ready")
        v_ready = sem("v_ready")
        qb_ready = sem("qb_ready")
        c_ready = sem("c_ready")
        less_ready = sem("less_ready")
        exp_done = sem("exp_done")
        dve_step = sem("dve_step")
        final_done = sem("final_done")
        tab_in = [sem(f"tab_in{h}") for h in range(2)]
        scored = sem("scored")
        copied_dve = sem("copied_dve")
        copied_act = sem("copied_act")
        stored = [sem(f"stored{r}") for r in range(RING)]

        block = ctx.enter_context(nc.Block())

        PAIRS = (NG - 2) // 2

        @block.sync
        def _(sp):
            sp.dma_start(w_sb[:, 0, :, :], w.rearrange("h (k d) -> h k d", k=K)).then_inc(loaded, 16)
            sp.dma_start(wt_sb[:, 0, :, :], w_t.rearrange("d (k h) -> d k h", k=K)).then_inc(loaded, 16)
            sp.dma_start(bias_sb[:, :], bias).then_inc(loaded, 16)
            sp.dma_start(ident_f[:, :], ident).then_inc(loaded, 16)
            sp.dma_start(slot_sb[:, :, :, :], slot_mask.rearrange("p (t s k) -> p t s k", s=SLOTS, k=K))\
              .then_inc(loaded, 16)
            for f in range(2):
                sp.dma_start(idx[f][:, :], index[f, :, :]).then_inc(idx_in[f], 16)
            with sp.Fori(0, NG // 2 - 1) as j:
                rows = sp.snap(16 * CHUNK * (j + 1))
                for h in range(2):
                    masks, nxt = sp.snap(2 * j + h + 1), sp.snap(2 * j + 2 + h)
                    for c in range(CHUNKS):
                        sp.wait_ge(gathered[h][c], rows)
                    sp.wait_ge(nz_done, masks)
                    sp.dma_start(idx[h][:, :], index[nxt, :, :]).then_inc(idx_in[h], 16)
            for h in range(2):
                sp.dma_start(tab[h][:, :], table_t[:, h * PIECE:(h + 1) * PIECE]).then_inc(tab_in[h], 16)

            def store(piece, h, m):
                n = (MT * NC // 2) * piece
                upto = NC * (m + 1)
                sp.compute_val(n + (upto + 1) // 2)
                sp.compute_val(n + upto // 2)
                sp.wait_ge(loaded, 16 * 5)
                sp.wait_ge(copied_dve, n + (upto + 1) // 2)
                sp.wait_ge(copied_act, n + upto // 2)
                sp.dma_start(out[m * P:(m + 1) * P, bass.ds(piece * PIECE, PIECE)], score[m % RING][:, :])\
                  .then_inc(stored[m % RING], 16)

            with sp.Fori(0, NP // 2 - 1) as j:
                for h in range(2):
                    for m in range(MT):
                        store(2 * j + h, h, m)
                    sp.dma_start(tab[h][:, :], table_t[:, bass.ds(PIECE * (2 * j + 2 + h), PIECE)])\
                      .then_inc(tab_in[h], 16)
            for h in range(2):
                for m in range(MT):
                    store(NP - 2 + h, h, m)
            for r in range(RING):
                sp.wait_ge(stored[r], 16 * (NP * MT // RING))

        @block.gpsimd
        def _(pool):
            pool.memset(ones_b[:, :], 1.0).then_inc(consts_done, 1)
            pool.memset(ones_f[:, :], 1.0).then_inc(consts_done, 1)
            pool.memset(zeros_b[:, :], 0.0).then_inc(consts_done, 1)

            def gather(h, use, routed=None):
                if routed is not None:
                    pool.compute_val(routed)
                    pool.compute_val(16 * (use + 1))
                    pool.wait_ge(loaded, 16 * 5)
                    pool.wait_ge(p_done, routed)
                pool.wait_ge(idx_in[h], 16 * (use + 1))
                for t in range(TILES):
                    pool.indirect_dma_start(
                        emb[h][:, t, :], None, table, bass.IndirectOffsetOnAxis(ap=idx[h][:, t:t + 1], axis=0),
                    ).then_inc(gathered[h][t // CHUNK], 16)

            gather(0, 0)
            gather(1, 0)
            with pool.Fori(0, NG // 2 - 1) as j:
                for h in range(2):
                    gather(h, j + 1, 3 * (2 * j + h + 1))

        @block.tensor
        def _(pe):
            def front(f, h, c):
                pe.wait_ge(split_done, CHUNKS * f + c + 1)
                for a in range(PARTS):
                    m = PARTS * c + a
                    slot = (PARTS * CHUNKS * h + m) % 2
                    if not (isinstance(f, int) and f == 0 and m < 2):
                        pe.wait_ge(et_copied, PARTS * CHUNKS * f + m - 1)
                    for i in range(CHUNK):
                        t = CHUNK * c + i
                        src = (upper(emb[h][:, t, :]), upper(rest[h][:, t, :]), low[h][:, t, :])[a]
                        last = nc.tensor.transpose(et_ps[slot][:, i * P:(i + 1) * P], src, ident_b[:, :])
                    last.then_inc(et_full, 1)

            def parts(h, t):
                return upper(emb[h][:, t, :]), upper(rest[h][:, t, :]), low[h][:, t, :]

            def pool_first(n, h):
                nc.tensor.matmul(p_ps[:, 0:PADG], ones_b[:, :], zeros_b[:, 0:PADG], start=True, stop=False)
                for t in range(TILES):
                    b = FIRST_SEQ[t]
                    for a, e in enumerate(parts(h, t)):
                        last = nc.tensor.matmul(p_ps[:, b:b + SLOTS], e, quarter[:, t, :],
                                                start=False, stop=(t == TILES - 1 and a == PARTS - 1))
                last.then_inc(p_done, 1)

            w3 = PARTS * PADG * K
            sums = p_ps[:, 0:w3].rearrange("p (a x) -> p a x", a=PARTS)
            counts = p_ps[:, w3:2 * w3].rearrange("p (a x) -> p a x", a=PARTS)

            def pool_weighted(n, h, it):
                pe.wait_ge(c_ready, 2 * n + it)
                nc.tensor.matmul(p_ps[:, 0:2 * w3], ones_b[:, :], zeros_b[:, :], start=True, stop=False)
                for t in range(TILES):
                    x = FIRST_SEQ[t] * K
                    c3 = upper(c_sb[:, :, t, :])
                    for e in parts(h, t):
                        nc.tensor.matmul(sums[:, :, x:x + SLOTS * K], e, c3, start=False, stop=False)
                    last = nc.tensor.matmul(counts[:, :, x:x + SLOTS * K], ones_b[:, :], c3,
                                            start=False, stop=(t == TILES - 1))
                last.then_inc(p_done, 1)

            def project(n, it):
                pe.wait_ge(pooled_ready, 3 * n + it + 1)
                for k in range(K):
                    if it == 0:
                        rhs = upper(pooled[:, 0:PARTS, 0:GROUP])
                    else:
                        rhs = upper(pooled[:, 0:PARTS, :]).rearrange("p a (b k) -> p a b k", k=K)[:, :, :, k]
                    for a in range(PARTS):
                        last = nc.tensor.matmul(s_out[:, k, :, :], wpart(w_sb, a, k), rhs,
                                                start=(a == 0), stop=(a == PARTS - 1))
                last.then_inc(s_done, 1)

            def wpart(t, a, k):
                return upper(t[:, a, k, :])

            def norms(n, it):
                pe.wait_ge(sq_ready, 4 * n + it + 1)
                nc.tensor.matmul(n_out, ones_f[:, :], sq[:, :], start=True, stop=True).then_inc(n_done, 1)

            def back(n, it):
                pe.wait_ge(v_ready, 2 * n + it + 1)
                for k in range(K):
                    rhs = upper(v_sb[:, :, :, :])[:, :, :, k]
                    for a in range(PARTS):
                        last = nc.tensor.matmul(q_out[:, k, :, :], wpart(wt_sb, a, k), rhs,
                                                start=(a == 0), stop=(a == PARTS - 1))
                last.then_inc(q_done, 1)

            def logits(n, h, it):
                pe.wait_ge(qb_ready, 2 * n + it + 1)
                for t in range(TILES):
                    x = FIRST_SEQ[t] * K
                    y = (t % HALF) * LW
                    to = l_ps[:, t // HALF, y:y + LW].rearrange("p (a x) -> p a x", a=PARTS)
                    q3 = upper(qb[:, :, :, :])
                    nc.tensor.matmul(to, ones_b[:, :], q3[:, :, 1, x:x + SLOTS * K], start=True, stop=False)
                    for a in range(PARTS):
                        last = nc.tensor.matmul(to, emb_t[h][:, a, t * P:(t + 1) * P], q3[:, :, 0, x:x + SLOTS * K],
                                                start=False, stop=(a == PARTS - 1))
                last.then_inc(l_done, 1)

            def body(i, h, has_front=True, has_chain=True):
                n, g = i - 1, 1 - h
                if has_chain:
                    pool_first(n, g)
                if has_front:
                    front(i, h, 0)
                if has_chain:
                    project(n, 0)
                    norms(n, 0)
                    back(n, 0)
                    pe.wait_ge(et_copied, PARTS * CHUNKS * (n + 1))
                    logits(n, g, 0)
                if has_front:
                    front(i, h, 1)
                if has_chain:
                    pool_weighted(n, g, 1)
                if has_front:
                    front(i, h, 2)
                if has_chain:
                    project(n, 1)
                    norms(n, 1)
                    back(n, 1)
                    logits(n, g, 1)
                if has_front:
                    front(i, h, 3)
                if has_chain:
                    pool_weighted(n, g, 2)
                if has_front:
                    front(i, h, 4)
                if has_chain:
                    project(n, 2)
                    norms(n, 2)
                    norms(n, 3)

            pe.wait_ge(consts_done, 3 + 6)
            body(0, 0, has_chain=False)
            with pe.Fori(0, PAIRS) as j:
                body(2 * j + 1, 1)
                body(2 * j + 2, 0)
            body(NG - 1, 1)
            body(NG, 0, has_front=False)

            pe.wait_ge(final_done, NG)

            def scores(piece, h, use):
                pe.wait_ge(tab_in[h], 16 * (use + 1))
                for m in range(MT):
                    for c in range(NC):
                        q = m * NC + c
                        if not (isinstance(piece, int) and piece == 0 and q < 2):
                            pe.wait_ge((copied_dve, copied_act)[q % 2], (MT * NC // 2) * piece + (q // 2))
                        nc.tensor.matmul(sc_ps[q % 2][:, 0:COLS], final_t[:, m * P:(m + 1) * P],
                                         tab[h][:, c * COLS:(c + 1) * COLS], start=True, stop=True).then_inc(scored, 1)

            scores(0, 0, 0)
            scores(1, 1, 0)
            with pe.Fori(1, NP // 2) as j:
                for h in range(2):
                    scores(2 * j + h, h, j)

        @block.scalar
        def _(act):
            def copy_out(f, h, c):
                for a in range(PARTS):
                    m = PARTS * c + a
                    slot = (PARTS * CHUNKS * h + m) % 2
                    act.wait_ge(et_full, PARTS * CHUNKS * f + m + 1)
                    nc.scalar.activation(emb_t[h][:, a, CHUNK * c * P:CHUNK * (c + 1) * P],
                                         et_ps[slot][:, 0:CHUNK * P], ACT.Copy).then_inc(et_copied, 1)

            def exponent(n, s):
                act.wait_ge(less_ready, 3 * n + s + 1)
                if s < 2:
                    nc.scalar.activation(ex[:, :, :], less[:, :, :], ACT.Exp).then_inc(exp_done, 1)
                else:
                    nc.scalar.activation(ex[:, 0:GROUP, :], less[:, 0:GROUP, :], ACT.Exp).then_inc(exp_done, 1)

            def body(i, h, has_front=True, has_chain=True):
                n = i - 1
                if has_front:
                    copy_out(i, h, 0)
                    copy_out(i, h, 1)
                if has_chain:
                    exponent(n, 0)
                if has_front:
                    copy_out(i, h, 2)
                    copy_out(i, h, 3)
                if has_chain:
                    exponent(n, 1)
                if has_front:
                    copy_out(i, h, 4)
                if has_chain:
                    exponent(n, 2)

            body(0, 0, has_chain=False)
            with act.Fori(0, PAIRS) as j:
                body(2 * j + 1, 1)
                body(2 * j + 2, 0)
            body(NG - 1, 1)
            body(NG, 0, has_front=False)

            def copies(piece):
                for m in range(MT):
                    for c in range(NC):
                        q = m * NC + c
                        if q % 2 == 0:
                            continue
                        if c < 2 and not (isinstance(piece, int) and piece == 0 and m < RING):
                            act.wait_ge(stored[m % RING], 16 * ((MT // RING) * piece + m // RING))
                        act.wait_ge(scored, MT * NC * piece + q + 1)
                        nc.scalar.activation(score[m % RING][:, c * COLS:(c + 1) * COLS], sc_ps[1][:, 0:COLS],
                                             ACT.Copy).then_inc(copied_act, 1)

            copies(0)
            with act.Fori(1, NP) as j:
                copies(j)

        @block.vector
        def _(dve):
            steps = [0]
            base = [0]

            def step(ins):
                steps[0] += 1
                ins.then_inc(dve_step, 1)
                dve.wait_ge(dve_step, base[0] + steps[0])

            def tt(o, a, b, op):
                return nc.vector.tensor_tensor(o, a, b, op)

            def split_words(word, a, b):
                return tt(b, a, word, ALU.subtract)

            dve.wait_ge(loaded, 16 * 5)
            for t in (w_sb, wt_sb):
                for a in range(2):
                    v = t[:, a, :, :].rearrange("p k n -> p (k n)")
                    step(tt(t[:, a + 1, :, :].rearrange("p k n -> p (k n)"), v, upper(v), ALU.subtract))
            nc.vector.tensor_copy(ident_b[:, :], ident_f[:, :]).then_inc(consts_done, 1)
            nc.vector.tensor_scalar(bias_n[:, :], bias_sb[:, :], float(SEQ) / K, None, ALU.mult).then_inc(consts_done, 1)
            nc.vector.tensor_scalar(quarter[:, :, :], slot_sb[:, :, :, 0], 1.0 / K, None, ALU.mult)\
              .then_inc(consts_done, 1)
            nc.vector.memset(nonzero[:, :], 0.0).then_inc(consts_done, 1)
            nc.vector.memset(qb[:, :, :, :], 0.0).then_inc(consts_done, 1)
            step(nc.vector.memset(l_ps[:, 1, (HALF - 1) * LW:HALF * LW], 0.0))
            nc.vector.memset(c_sb[:, :, :, :], 0.0).then_inc(consts_done, 1)
            dve.wait_ge(consts_done, 9)

            def front(f, h, use, c):
                if c == 0:
                    dve.wait_ge(idx_in[h], 16 * (use + 1))
                    nc.vector.tensor_scalar(nonzero[:, 0:TILES], idx[h][:, :].bitcast(I32), 0.0, None, ALU.not_equal)\
                      .then_inc(nz_done, 1)
                    dve.wait_ge(nz_done, f + 1)
                    nc.vector.tensor_tensor(
                        mask[h][:, :, :, :].rearrange("p t s k -> p t (s k)"),
                        slot_sb[:, :, :, :].rearrange("p t s k -> p t (s k)"),
                        nonzero[:, :].unsqueeze(2).to_broadcast([P, PADT, SLOTS * K]), ALU.mult)
                dve.wait_ge(gathered[h][c], 16 * CHUNK * (use + 1))
                t0, t1 = CHUNK * c, CHUNK * (c + 1)
                e = emb[h][:, t0:t1, :].rearrange("p t n -> p (t n)")
                r = rest[h][:, t0:t1, :].rearrange("p t n -> p (t n)")
                step(tt(r, e, upper(e), ALU.subtract))
                tt(low[h][:, t0:t1, :].rearrange("p t n -> p (t n)"), r, upper(r), ALU.subtract)\
                    .then_inc(split_done, 1)

            def pooled_parts(n, it):
                dve.wait_ge(p_done, 3 * n + it + 1)
                width = GROUP if it == 0 else GK
                if it == 0:
                    step(nc.vector.tensor_copy(pooled[:, 0, 0:GROUP], p_ps[:, 0:GROUP]))
                else:
                    w3 = PARTS * PADG * K
                    view = p_ps[:, 0:2 * w3].rearrange("p (s a x) -> p s x a", s=2, a=PARTS)[:, :, 0:GK, :]
                    step(nc.vector.tensor_reduce(pooled[:, 0:PARTS + 1:PARTS, :], view, AX.X, ALU.add))
                step(tt(pooled[:, 1, 0:width], pooled[:, 0, 0:width], upper(pooled[:, 0, 0:width]), ALU.subtract))
                tt(pooled[:, 2, 0:width], pooled[:, 1, 0:width], upper(pooled[:, 1, 0:width]), ALU.subtract)\
                    .then_inc(pooled_ready, 1)
                if it:
                    tt(count_b[:, :, :], pooled[:, PARTS, :].rearrange("p (b k) -> p b k", k=K),
                       bias_sb[:, :].unsqueeze(1).to_broadcast([P, GROUP, K]), ALU.mult)

            def squash(n, it):
                dve.wait_ge(s_done, 3 * n + it + 1)
                step(nc.vector.tensor_reduce(s_sb[:, :, :].rearrange("p b k -> p k b"),
                                             s_out.rearrange("p k a b -> p k b a"), AX.X, ALU.add))
                share = count_b[:, :, :] if it else bias_n[:, :].unsqueeze(1).to_broadcast([P, GROUP, K])
                step(tt(s_sb[:, :, :], s_sb[:, :, :], share, ALU.add))
                s = s_sb[:, :, :].rearrange("p b k -> p (b k)")
                tt(sq[:, :], s, s, ALU.mult).then_inc(sq_ready, 1)
                dve.wait_ge(n_done, 4 * n + it + 1)
                step(nc.vector.tensor_copy(n2[:, :], n_out))
                step(nc.vector.tensor_scalar(guess[:, :], n2[:, :].bitcast(I32), -0.5, RSQRT_MAGIC, ALU.mult, ALU.add))
                r, spare = guess[:, :].bitcast(F32), td
                for newton in range(3):
                    step(tt(ta[:, :], n2[:, :], r, ALU.mult))
                    step(nc.vector.scalar_tensor_tensor(tb[:, :], ta[:, :], -0.5, r, ALU.mult, ALU.mult))
                    o = (tc, td, tc)[newton][:, :]
                    step(nc.vector.scalar_tensor_tensor(o, tb[:, :], 1.5, r if newton < 2 else ta[:, :],
                                                        ALU.add, ALU.mult))
                    r = o
                step(nc.vector.tensor_scalar(ta[:, :], r, 1e-12, None, ALU.add))
                step(nc.vector.scalar_tensor_tensor(tb[:, :], n2[:, :], 1.0, ta[:, :], ALU.add, ALU.mult))
                step(nc.vector.reciprocal(ta[:, :], tb[:, :]))
                step(tt(tb[:, :], n2[:, :], ta[:, :], ALU.mult))
                v = [v_sb[:, a, :, :].rearrange("p b k -> p (b k)") for a in range(PARTS)]
                step(tt(v[0], s, tb[:, :], ALU.mult))
                if it < 2:
                    step(tt(v[1], v[0], upper(v[0]), ALU.subtract))
                    tt(v[2], v[1], upper(v[1]), ALU.subtract).then_inc(v_ready, 1)
                    tt(qb[:, 0, 1, 0:GK].rearrange("p (b k) -> p b k", k=K), v_sb[:, 0, :, :],
                       bias_sb[:, :].unsqueeze(1).to_broadcast([P, GROUP, K]), ALU.mult)

            def back_parts(n, it):
                dve.wait_ge(q_done, 2 * n + it + 1)
                step(nc.vector.tensor_reduce(qb[:, 0, 0, 0:GK].rearrange("p (b k) -> p k b", k=K),
                                             q_out.rearrange("p k a b -> p k b a"), AX.X, ALU.add))
                q = [qb[:, a, :, :].rearrange("p s x -> p (s x)") for a in range(PARTS)]
                step(tt(q[1], q[0], upper(q[0]), ALU.subtract))
                tt(q[2], q[1], upper(q[1]), ALU.subtract).then_inc(qb_ready, 1)

            def softmax(n, s, x, rows):
                bc = lambda t: t[:, 0:rows].unsqueeze(2).to_broadcast([P, rows, K])
                step(nc.vector.tensor_reduce(top[:, 0:rows], x, AX.X, ALU.max))
                tt(less[:, 0:rows, :], x, bc(top), ALU.subtract).then_inc(less_ready, 1)
                dve.wait_ge(exp_done, 3 * n + s + 1)
                step(nc.vector.tensor_reduce(total[:, 0:rows], ex[:, 0:rows, :], AX.X, ALU.add))
                step(nc.vector.reciprocal(inv[:, 0:rows], total[:, 0:rows]))
                step(tt(prob[:, 0:rows, :], ex[:, 0:rows, :], bc(inv), ALU.mult))

            def weights(n, h, it):
                dve.wait_ge(l_done, 2 * n + it + 1)
                flat = "p t s k -> p (t s k)"
                step(nc.vector.tensor_reduce(
                    summed[:, :, :, :].rearrange("p (u t) s k -> p u t (s k)", u=2),
                    l_ps[:, :, 0:HALF * LW].rearrange("p u (t a x) -> p u t x a", t=HALF, a=PARTS), AX.X, ALU.add))
                step(tt(masked[:, :, :, :].rearrange(flat), summed[:, :, :, :].rearrange(flat),
                        mask[h][:, :, :, :].rearrange(flat), ALU.mult))
                to = (logit, delta)[it]
                step(tt(to[:, :, :], masked[:, :, 0, :], masked[:, :, 1, :], ALU.add))
                if it:
                    step(tt(logit[:, :, :], logit[:, :, :], delta[:, :, :], ALU.add))
                softmax(n, it, logit[:, :, :], PADT)
                c = [c_sb[:, a, :, :].rearrange("p t x -> p (t x)") for a in range(PARTS)]
                step(tt(c_sb[:, 0, :, :].rearrange("p t (s k) -> p t s k", k=K), slot_sb[:, :, :, :],
                        prob[:, :, :].unsqueeze(2).to_broadcast([P, PADT, SLOTS, K]), ALU.mult))
                step(tt(c[1], c[0], upper(c[0]), ALU.subtract))
                tt(c[2], c[1], upper(c[1]), ALU.subtract).then_inc(c_ready, 1)

            def finish(n, h):
                step(nc.vector.tensor_reduce(
                    last_t[:, :], emb_t[h][:, :, SEQ - 1:TILES * P:SEQ].rearrange("p a b -> p b a"), AX.X, ALU.add))
                tt(sq[:, :].rearrange("p (b k) -> p b k", k=K), v_sb[:, 0, :, :],
                   last_t[:, :].unsqueeze(2).to_broadcast([P, GROUP, K]), ALU.mult).then_inc(sq_ready, 1)
                dve.wait_ge(n_done, 4 * n + 4)
                step(nc.vector.tensor_copy(n2[:, :], n_out))
                softmax(n, 2, n2[:, :].rearrange("p (b k) -> p b k", k=K), GROUP)
                step(tt(ta[:, :].rearrange("p (b k) -> p b k", k=K), prob[:, 0:GROUP, :], v_sb[:, 0, :, :], ALU.mult))
                nc.vector.tensor_reduce(final_t[:, bass.ds(n * GROUP, GROUP)],
                                        ta[:, :].rearrange("p (b k) -> p b k", k=K), AX.X, ALU.add)\
                  .then_inc(final_done, 1)

            def body(i, h, use, count, has_front=True, has_chain=True):
                n, g = i - 1, 1 - h
                base[0], steps[0] = count, 0
                if has_front:
                    front(i, h, use, 0)
                if has_chain:
                    pooled_parts(n, 0)
                    squash(n, 0)
                    back_parts(n, 0)
                if has_front:
                    front(i, h, use, 1)
                if has_chain:
                    weights(n, g, 0)
                if has_front:
                    front(i, h, use, 2)
                if has_chain:
                    pooled_parts(n, 1)
                    squash(n, 1)
                    back_parts(n, 1)
                if has_front:
                    front(i, h, use, 3)
                if has_chain:
                    weights(n, g, 1)
                if has_front:
                    front(i, h, use, 4)
                if has_chain:
                    pooled_parts(n, 2)
                    squash(n, 2)
                    finish(n, g)
                return steps[0]

            before = steps[0]
            first = body(0, 0, 0, before, has_chain=False)
            each = BODY_STEPS
            with dve.Fori(0, PAIRS) as j:
                a = body(2 * j + 1, 1, j, before + first + 2 * each * j)
                b = body(2 * j + 2, 0, j + 1, before + first + 2 * each * j + each)
            assert a == b == each, (a, b)
            done = before + first + 2 * each * PAIRS
            body(NG - 1, 1, NG // 2 - 1, done)
            body(NG, 0, 0, done + each, has_front=False)

            def copies(piece):
                for m in range(MT):
                    for c in range(NC):
                        q = m * NC + c
                        if q % 2:
                            continue
                        if c < 2 and not (isinstance(piece, int) and piece == 0 and m < RING):
                            dve.wait_ge(stored[m % RING], 16 * ((MT // RING) * piece + m // RING))
                        dve.wait_ge(scored, MT * NC * piece + q + 1)
                        nc.vector.tensor_copy(score[m % RING][:, c * COLS:(c + 1) * COLS], sc_ps[0][:, 0:COLS])\
                          .then_inc(copied_dve, 1)

            copies(0)
            with dve.Fori(1, NP) as j:
                copies(j)


BODY_STEPS = 97


def kernel(r_seq, L0_rec_emb_table, L0_rec_s_w, L0_rec_s_b):
    import concourse.bacc as bacc
    from concourse.bass_utils import run_bass_kernel_spmd

    r_seq, table, w, b = (np.asarray(x) for x in (r_seq, L0_rec_emb_table, L0_rec_s_w, L0_rec_s_b))
    position = np.arange(TILES * P).reshape(TILES, P).T
    slot = np.zeros((P, PADT, SLOTS, K), np.float32)
    for s in range(SLOTS):
        slot[:, :TILES, s, :] = (position // SEQ == np.array(FIRST_SEQ) + s)[:, :, None]
    arrays = {
        "index": np.ascontiguousarray(r_seq.reshape(NG, TILES, P).transpose(0, 2, 1)).view(np.uint32),
        "table": np.ascontiguousarray(table),
        "table_t": np.ascontiguousarray(table.T),
        "w": np.ascontiguousarray(w),
        "w_t": np.ascontiguousarray(w.reshape(HID, K, HID).transpose(2, 1, 0).reshape(HID, K * HID)),
        "bias": np.ascontiguousarray(b.reshape(K, HID).T),
        "ident": np.eye(P, dtype=np.float32),
        "slot_mask": slot.reshape(P, -1),
    }
    nc = bacc.Bacc("TRN2", target_bir_lowering=False, num_devices=1)
    args = [nc.dram_tensor(n, a.shape, mybir.dt.from_np(a.dtype), kind="ExternalInput").ap() for n, a in arrays.items()]
    out = nc.dram_tensor("scores", (BATCH, ITEMS), F32, kind="ExternalOutput").ap()
    build(nc, *args, out)
    r = run_bass_kernel_spmd(nc, [arrays], core_ids=[0])
    return r.results[0]["scores"]
```

```python
from contextlib import ExitStack

import numpy as np

import concourse.bass as bass
from concourse import mybir

F32 = mybir.dt.float32
BF16 = mybir.dt.bfloat16
I32 = mybir.dt.int32
U32 = mybir.dt.uint32
ALU = mybir.AluOpType
ACT = mybir.ActivationFunctionType
AX = mybir.AxisListType

P = 128
BATCH, SEQ, K, HID, ITEMS = 1024, 200, 4, 128, 100000
GROUP = 16
TILES = GROUP * SEQ // P
NG = BATCH // GROUP
PADT = TILES + 1
HALF = PADT // 2
PADG = GROUP + 1
SLOTS = 2
PARTS = 3
LANES = 3
CHUNK = 5
CHUNKS = TILES // CHUNK
GK = GROUP * K
SK = SLOTS * K
LW = PARTS * SK
PW = PARTS * PADG * K
NORM_ROWS = LANES * GK // 2
BUFS = 3
AHEAD = 2
RSQRT_MAGIC = 1597463007.0

MT = 4
PIECE = 800
COLS = 400
SPLITS = PIECE // COLS
NPIECE = ITEMS // PIECE
RING = 4
PER_PIECE = MT * SPLITS
FIRST_SCORE = 36
LAST_BODY = NG + LANES - 1
FILL = (4, 2, 5, 3, 2, 16)
assert sum(FILL) == RING * PER_PIECE
IN_BODIES = (LAST_BODY - FIRST_SCORE + 1) * RING

FIRST_SEQ = [P * t // SEQ for t in range(TILES)]


def upper(ap):
    names = " ".join("abcd"[: len(ap.shape) - 2])
    v = ap.bitcast(BF16)
    return v.rearrange(f"p {names} (n two) -> p {names} n two", two=2)[..., 1]


def build(nc, index, table, table_t, w, w_t, bias, bias_rows, ident, slot_mask, out):
    ctx = ExitStack()
    with ctx:
        def sb(name, shape, dt=F32):
            return ctx.enter_context(nc.sbuf_tensor(name, shape, dt))

        def ps(name, shape, dt=F32):
            return ctx.enter_context(nc.psum_tensor(name, shape, dt))

        def sem(name):
            return ctx.enter_context(nc.semaphore(name))

        idx = [sb(f"idx{b}", [P, TILES], U32) for b in range(BUFS)]
        emb = sb("emb", [P, TILES, HID])
        rest = [sb(f"rest{r}", [P, CHUNK * HID]) for r in range(2)]
        nat = [sb(f"nat{b}", [P, PARTS, TILES, HID], BF16) for b in range(BUFS)]
        emb_t = [sb(f"emb_t{b}", [P, PARTS, TILES * P], BF16) for b in range(BUFS)]
        mask = [sb(f"mask{b}", [P, PADT, SK]) for b in range(BUFS)]
        w_sb = sb("w_sb", [P, PARTS, K, HID], BF16)
        wt_sb = sb("wt_sb", [P, PARTS, K, HID], BF16)
        bias_sb = sb("bias_sb", [P, K])
        brow = sb("brow", [P, K * HID], BF16)
        ident_f = sb("ident_f", [P, P])
        ident_b = sb("ident_b", [P, P], BF16)
        ones_b = sb("ones_b", [P, P], BF16)
        ones_f = sb("ones_f", [P, P])
        zeros_b = sb("zeros_b", [P, 2 * PW], BF16)
        slot_sb = sb("slot_sb", [P, PADT, SK])
        quarter = sb("quarter", [P, PADT, SLOTS], BF16)
        nonzero = sb("nonzero", [P, PADT])
        pooled = sb("pooled", [P, PARTS, 2, LANES * GK])
        s_sb = sb("s_sb", [P, LANES * GK])
        sq = sb("sq", [P, LANES * GK])
        rs = [sb(f"rs{i}", [P, 2]) for i in range(8)]
        guess = sb("guess", [P, 2], I32)
        diag = sb("diag", [P, 2, NORM_ROWS])
        v_sb = sb("v_sb", [P, PARTS, LANES * GK])
        qb = sb("qb", [P, PARTS, 2, 2, PADG * K])
        summed = sb("summed", [P, 2, PADT, SK])
        masked = sb("masked", [P, 2, PADT, SK])
        logit = sb("logit", [P, 2, PADT, K])
        before = sb("before", [P, PADT, K])
        top = sb("top", [P, 2 * PADT])
        less = sb("less", [P, 2 * PADT, K])
        ex = sb("ex", [P, 2 * PADT, K])
        own = sb("own", [P, 2 * PADT, SK])
        total = sb("total", [P, 2 * PADT])
        inv = sb("inv", [P, 2 * PADT])
        c_sb = sb("c_sb", [P, 2, PARTS, PADT * SK])
        last_t = sb("last_t", [P, GROUP])
        att = sb("att", [P, GROUP, K])
        att_top = sb("att_top", [P, GROUP])
        att_less = sb("att_less", [P, GROUP, K])
        att_ex = sb("att_ex", [P, GROUP, K])
        att_total = sb("att_total", [P, GROUP])
        att_sum = sb("att_sum", [P, GROUP])
        final_t = sb("final_t", [P, BATCH])
        tab = [sb(f"tab{r}", [P, PIECE]) for r in range(RING)]
        score = [sb(f"score{m}", [P, PIECE]) for m in range(MT)]

        et_ps = [ps(f"et_ps{i}", [P, 2 * 512], BF16) for i in range(2)]
        l_ps = ps("l_ps", [P, 2, 512])
        pa_ps = ps("pa_ps", [P, 512])
        pb_ps = ps("pb_ps", [P, 512])
        sc_ps = [ps(f"sc_ps{i}", [P, 512]) for i in range(2)]
        LB = LANES * GROUP
        s_out = l_ps[:, :, 0:2 * PARTS * LB].rearrange("p u (k a x) -> p u k a x", k=2, a=PARTS)
        q_out = l_ps[:, :, 0:2 * PARTS * 2 * GROUP].rearrange("p u (k a x) -> p u k a x", k=2, a=PARTS)
        first_out = pa_ps[:, 2 * PW:2 * PW + PADG]
        factor_out = pa_ps[:, 0:LANES * GK]
        norm_out = pb_ps[0:NORM_ROWS, 0:2]
        att_out = pb_ps[:, 64:64 + GK]

        loaded = sem("loaded")
        made = sem("made")
        idx_in = [sem(f"idx_in{b}") for b in range(BUFS)]
        gathered = [sem(f"gathered{c}") for c in range(CHUNKS)]
        nz_done = sem("nz_done")
        first_copied = sem("first_copied")
        rest_done = sem("rest_done")
        mid_copied = sem("mid_copied")
        low_done = sem("low_done")
        et_full = sem("et_full")
        et_copied = sem("et_copied")
        p_done = [sem(f"p_done{n}") for n in range(LANES)]
        pooled_ready = sem("pooled_ready")
        s_done = sem("s_done")
        sq_ready = sem("sq_ready")
        n_done = sem("n_done")
        diag_ready = sem("diag_ready")
        f_done = sem("f_done")
        v_ready = sem("v_ready")
        q_done = sem("q_done")
        qb_ready = sem("qb_ready")
        l_done = [[sem(f"l_done{n}_{u}") for u in range(2)] for n in range(2)]
        l_read = [sem(f"l_read{u}") for u in range(2)]
        less_ready = sem("less_ready")
        exp_done = sem("exp_done")
        c_ready = sem("c_ready")
        prod_ready = sem("prod_ready")
        a_done = sem("a_done")
        att_less_ready = sem("att_less_ready")
        att_exp_done = sem("att_exp_done")
        last_read = sem("last_read")
        final_done = sem("final_done")
        dve_step = sem("dve_step")
        tab_in = [sem(f"tab_in{r}") for r in range(RING)]
        scored = sem("scored")
        copied = sem("copied")
        stored = [sem(f"stored{m}") for m in range(MT)]

        LOADS, MADE_BY_POOL = 7, 3
        block = ctx.enter_context(nc.Block())

        def active(i, lane):
            return not isinstance(i, int) or 0 <= i - 1 - lane < NG

        @block.sync
        def _(sp):
            sp.dma_start(tab[0][:, 0:K * HID], w).then_inc(loaded, 16)
            sp.dma_start(tab[1][:, 0:K * HID], w_t).then_inc(loaded, 16)
            sp.dma_start(bias_sb[:, :], bias).then_inc(loaded, 16)
            sp.dma_start(tab[3][0:PARTS, 0:K * HID], bias_rows).then_inc(loaded, 16)
            sp.dma_start(ident_f[:, :], ident).then_inc(loaded, 16)
            sp.dma_start(slot_sb[:, :, :], slot_mask.rearrange("p (t x) -> p t x", x=SK)).then_inc(loaded, 16)
            for b in range(BUFS):
                sp.dma_start(idx[b][:, :], index[b, :, :]).then_inc(idx_in[b], 16)

            def indices(f, b):
                sp.compute_val(16 * CHUNK * (f - BUFS + 1))
                sp.compute_val(f - BUFS + 1)
                sp.wait_ge(loaded, 16 * (LOADS - 1))
                for c in range(CHUNKS):
                    sp.wait_ge(gathered[c], 16 * CHUNK * (f - BUFS + 1))
                sp.wait_ge(nz_done, f - BUFS + 1)
                sp.dma_start(idx[b][:, :], index[f, :, :]).then_inc(idx_in[b], 16)

            def load(q, r):
                item = q if isinstance(q, int) and q < NPIECE else q - NPIECE if isinstance(q, int) else q
                sp.dma_start(tab[r][:, :], table_t[:, bass.ds(item * PIECE, PIECE)]).then_inc(tab_in[r], 16)

            def stores(q, r, half, item):
                for m in range(MT):
                    row = (half * MT + m) * P
                    sp.compute_val(PER_PIECE * q + SPLITS * (m + 1))
                    sp.wait_ge(loaded, 16 * (LOADS - 1))
                    sp.wait_ge(copied, PER_PIECE * q + SPLITS * (m + 1))
                    sp.dma_start(out[row:row + P, bass.ds(item * PIECE, PIECE)], score[m][:, :])\
                      .then_inc(stored[m], 16)

            sp.wait_ge(made, MADE_BY_POOL + 1)
            for r in range(RING):
                load(r, r)

            def of_body(i, b):
                if not isinstance(i, int) or i + AHEAD < NG:
                    indices(i + AHEAD, (b + AHEAD) % BUFS)
                for r in range(RING):
                    q = RING * (i - FIRST_SCORE) + r
                    stores(q, r, 0, q)
                    load(q + RING, r)

            with sp.Fori(1, FIRST_SCORE // BUFS) as j:
                for b in range(BUFS):
                    indices(BUFS * j + b, b)
            for f in range(FIRST_SCORE, FIRST_SCORE + AHEAD):
                indices(f, f % BUFS)
            looped = (NG - AHEAD) // BUFS
            with sp.Fori(FIRST_SCORE // BUFS, looped) as j:
                for b in range(BUFS):
                    of_body(BUFS * j + b, b)
            for i in range(BUFS * looped, LAST_BODY):
                of_body(i, i % BUFS)
            for q in range(IN_BODIES - RING, NPIECE + RING - 1):
                stores(q, q % RING, q // NPIECE, q % NPIECE)
                load(q + RING, q % RING)
            first = NPIECE + RING - 1
            assert first % RING == 0
            rounds = (2 * NPIECE - first) // RING
            left = 2 * NPIECE - first - RING * rounds
            with sp.Fori(0, rounds - 1) as j:
                for r in range(RING):
                    item = RING * j + (first - NPIECE) + r
                    stores(RING * j + first + r, r, 1, item)
                    sp.dma_start(tab[r][:, :], table_t[:, bass.ds((item + RING) * PIECE, PIECE)]).then_inc(tab_in[r], 16)
            for q in range(first + RING * (rounds - 1), 2 * NPIECE):
                stores(q, q % RING, 1, q - NPIECE)
                if q + RING < 2 * NPIECE:
                    load(q + RING, q % RING)
            for m in range(MT):
                sp.wait_ge(stored[m], 16 * 2 * NPIECE)

        @block.gpsimd
        def _(pool):
            pool.memset(ones_b[:, :], 1.0).then_inc(made, 1)
            pool.memset(ones_f[:, :], 1.0).then_inc(made, 1)
            pool.memset(zeros_b[:, :], 0.0).then_inc(made, 1)

            def gather(f, b, use):
                for c in range(CHUNKS):
                    if not (isinstance(f, int) and f == 0):
                        pool.compute_val(CHUNKS * (f - 1) + c + 1)
                        pool.compute_val(16 * (use + 1))
                        pool.wait_ge(loaded, 16)
                        pool.wait_ge(first_copied, CHUNKS * (f - 1) + c + 1)
                        pool.wait_ge(rest_done, CHUNKS * (f - 1) + c + 1)
                    if c == 0:
                        pool.wait_ge(idx_in[b], 16 * (use + 1))
                    for t in range(CHUNK * c, CHUNK * (c + 1)):
                        pool.indirect_dma_start(
                            emb[:, t, :], None, table, bass.IndirectOffsetOnAxis(ap=idx[b][:, t:t + 1], axis=0),
                        ).then_inc(gathered[c], 16)

            for f in range(BUFS):
                gather(f, f, 0)
            with pool.Fori(1, NG // BUFS) as j:
                for b in range(BUFS):
                    gather(BUFS * j + b, b, j)
            gather(NG - 1, (NG - 1) % BUFS, (NG - 1) // BUFS)

        @block.tensor
        def _(pe):
            at = [0]

            def fill(q0, use, count):
                for s in range(at[0], at[0] + count):
                    p, s = divmod(s, PER_PIECE)
                    m, c = divmod(s, SPLITS)
                    product(q0 + p, p, use, 0, m, c)
                at[0] += count

            def product(q, r, use, half, m, c):
                if m == 0 and c == 0:
                    pe.wait_ge(tab_in[r], 16 * (use + 1))
                s = PER_PIECE * q + SPLITS * m + c
                if not (isinstance(s, int) and s < 2):
                    pe.wait_ge(copied, s - 1)
                nc.tensor.matmul(sc_ps[c][:, 0:COLS], final_t[:, (half * MT + m) * P:(half * MT + m + 1) * P],
                                 tab[r][:, c * COLS:(c + 1) * COLS], start=True, stop=True).then_inc(scored, 1)

            def front(f, b, c):
                for a, (ready) in enumerate((first_copied, mid_copied, low_done)):
                    pe.wait_ge(ready, CHUNKS * f + c + 1)
                    m = PARTS * c + a
                    if m >= 2:
                        pe.wait_ge(et_copied, PARTS * CHUNKS * f + m - 1)
                    elif m == 0 and not (isinstance(f, int) and f == 0):
                        pe.wait_ge(et_copied, PARTS * CHUNKS * f)
                    for n in range(CHUNK):
                        last = nc.tensor.transpose(et_ps[m % 2][:, n * P:(n + 1) * P],
                                                   nat[b][:, a, CHUNK * c + n, :], ident_b[:, :])
                    last.then_inc(et_full, 1)

            def sum_first(b):
                nc.tensor.matmul(first_out, ones_b[:, :], zeros_b[:, 0:PADG], start=True, stop=False)
                for t in range(TILES):
                    x = FIRST_SEQ[t]
                    for a in range(PARTS):
                        last = nc.tensor.matmul(first_out[:, x:x + SLOTS], nat[b][:, a, t, :], quarter[:, t, :],
                                                start=False, stop=(t == TILES - 1 and a == PARTS - 1))
                last.then_inc(p_done[0], 1)

            def sum_weighted(b, lane, bank):
                nc.tensor.matmul(bank[:, 0:2 * PW], ones_b[:, :], zeros_b[:, :], start=True, stop=False)
                sums, counts = (bank[:, s * PW:(s + 1) * PW].rearrange("p (a x) -> p a x", a=PARTS) for s in range(2))
                for t in range(TILES):
                    x = FIRST_SEQ[t] * K
                    c3 = upper(c_sb[:, lane - 1, :, t * SK:(t + 1) * SK])
                    for a in range(PARTS):
                        nc.tensor.matmul(sums[:, :, x:x + SK], nat[b][:, a, t, :], c3, start=False, stop=False)
                    last = nc.tensor.matmul(counts[:, :, x:x + SK], ones_b[:, :], c3,
                                            start=False, stop=(t == TILES - 1))
                last.then_inc(p_done[lane], 1)

            def logits(b, lane, u):
                for t in range(HALF * u, min(HALF * (u + 1), TILES)):
                    x = FIRST_SEQ[t] * K
                    y = (t - HALF * u) * LW
                    to = l_ps[:, u, y:y + LW].rearrange("p (a x) -> p a x", a=PARTS)
                    own_q, own_b = (upper(qb[:, :, s, lane, x:x + SK]) for s in range(2))
                    nc.tensor.matmul(to, ones_b[:, :], own_b, start=True, stop=False)
                    for a in range(PARTS):
                        last = nc.tensor.matmul(to, emb_t[b][:, a, t * P:(t + 1) * P], own_q,
                                                start=False, stop=(a == PARTS - 1))
                last.then_inc(l_done[lane][u], 1)

            def body(i, b, loop=None, scores=False):
                at[0] = 0
                q0 = RING * (i - FIRST_SCORE) if scores else 0
                gap = (lambda n: fill(q0, i - FIRST_SCORE, FILL[n])) if scores else (lambda n: None)
                has_front = not isinstance(i, int) or i < NG
                group_buf = [(b - 1 - lane) % BUFS for lane in range(LANES)]
                if isinstance(i, int) and i == 0:
                    for c in range(CHUNKS):
                        front(i, b, c)
                    return
                if active(i, 0):
                    sum_first(group_buf[0])
                if active(i, 1) or active(i, 2):
                    pe.wait_ge(c_ready, i - 1)
                if active(i, 2):
                    sum_weighted(group_buf[2], 2, pb_ps)
                if active(i, 1):
                    sum_weighted(group_buf[1], 1, pa_ps)
                if has_front:
                    front(i, b, 0)
                gap(0)
                pe.wait_ge(pooled_ready, i)
                for k in range(K):
                    to = s_out[:, k // 2, k % 2, :, :]
                    part = [pooled[:, :, s, :].bitcast(BF16).rearrange("p a (x k two) -> p a x k two", k=K, two=2)
                            [:, :, :, k, 1] for s in range(2)]
                    for a in range(PARTS):
                        nc.tensor.matmul(to, w_sb[:, a, k, :], part[0], start=(a == 0), stop=False)
                    last = nc.tensor.matmul(to, brow[:, k * HID:(k + 1) * HID], part[1], start=False, stop=True)
                last.then_inc(s_done, 1)
                gap(1)
                pe.wait_ge(sq_ready, i)
                for n in range(2):
                    last = nc.tensor.matmul(norm_out[:, n:n + 1], sq[:, n * NORM_ROWS:(n + 1) * NORM_ROWS],
                                            ones_f[:, 0:1], start=True, stop=True)
                last.then_inc(n_done, 1)
                if has_front:
                    front(i, b, 1)
                gap(2)
                pe.wait_ge(diag_ready, i)
                for n in range(2):
                    last = nc.tensor.matmul(factor_out[:, n * NORM_ROWS:(n + 1) * NORM_ROWS],
                                            ones_f[0:NORM_ROWS, :], diag[0:NORM_ROWS, n, :], start=True, stop=True)
                last.then_inc(f_done, 1)
                gap(3)
                routed = active(i, 0) or active(i, 1)
                if routed:
                    pe.wait_ge(v_ready, i)
                    for k in range(K):
                        v3 = v_sb[:, :, 0:2 * GK].bitcast(BF16)\
                            .rearrange("p a (x k two) -> p a x k two", k=K, two=2)[:, :, :, k, 1]
                        for a in range(PARTS):
                            last = nc.tensor.matmul(q_out[:, k // 2, k % 2, :, :], wt_sb[:, a, k, :], v3,
                                                    start=(a == 0), stop=(a == PARTS - 1))
                    last.then_inc(q_done, 1)
                if has_front:
                    front(i, b, 2)
                gap(4)
                if active(i, 2):
                    pe.wait_ge(prod_ready, i - 2)
                    nc.tensor.matmul(att_out, ones_f[:, :], att[:, :, :].rearrange("p b k -> p (b k)"),
                                     start=True, stop=True).then_inc(a_done, 1)
                if routed:
                    pe.wait_ge(qb_ready, i)
                if active(i, 1):
                    for u in range(2):
                        logits(group_buf[1], 1, u)
                if has_front:
                    front(i, b, 3)
                if active(i, 0):
                    pe.wait_ge(et_copied, PARTS * CHUNKS * i)
                    for u in range(2):
                        if active(i, 1):
                            pe.wait_ge(l_read[u], i - 1)
                        logits(group_buf[0], 0, u)
                if has_front:
                    front(i, b, 4)
                gap(5)

            pe.wait_ge(made, MADE_BY_POOL + 1)

            def run_pe():
                for i in range(BUFS):
                    body(i, i)
                with pe.Fori(1, FIRST_SCORE // BUFS) as j:
                    for b in range(BUFS):
                        body(BUFS * j + b, b)
                pe.wait_ge(final_done, NG // 2)
                for i in range(FIRST_SCORE, FIRST_SCORE + BUFS):
                    body(i, i % BUFS, scores=True)
                with pe.Fori(FIRST_SCORE // BUFS + 1, NG // BUFS) as j:
                    for b in range(BUFS):
                        body(BUFS * j + b, b, scores=True)
                for i in range(NG // BUFS * BUFS, LAST_BODY + 1):
                    body(i, i % BUFS, scores=True)

            run_pe()

            def piece(q, r, use, half):
                for m in range(MT):
                    for c in range(SPLITS):
                        product(q, r, use, half, m, c)

            for q in range(IN_BODIES, NPIECE):
                piece(q, q % RING, q // RING, 0)
            pe.wait_ge(final_done, NG)
            first = NPIECE + RING - 1
            for q in range(NPIECE, first):
                piece(q, q % RING, q // RING, 1)
            rounds = (2 * NPIECE - first) // RING
            with pe.Fori(0, rounds) as j:
                for r in range(RING):
                    piece(RING * j + first + r, r, j + first // RING, 1)
            for q in range(first + RING * rounds, 2 * NPIECE):
                piece(q, q % RING, q // RING, 1)

        @block.scalar
        def _(act):
            at = [0]

            def copy_scores(q, m, c):
                if c == 0 and not (isinstance(q, int) and q == 0):
                    act.wait_ge(stored[m], 16 * q)
                act.wait_ge(scored, PER_PIECE * q + SPLITS * m + c + 1)
                nc.scalar.activation(score[m][:, c * COLS:(c + 1) * COLS], sc_ps[c][:, 0:COLS], ACT.Copy)\
                    .then_inc(copied, 1)

            def fill(q0, count):
                for s in range(at[0], at[0] + count):
                    p, s = divmod(s, PER_PIECE)
                    copy_scores(q0 + p, *divmod(s, SPLITS))
                at[0] += count

            def parts(f, b, c):
                t0, t1 = CHUNK * c, CHUNK * (c + 1)
                flat = "p t n -> p (t n)"
                act.wait_ge(gathered[c], 16 * CHUNK * (f + 1))
                nc.scalar.activation(nat[b][:, 0, t0:t1, :].rearrange(flat), upper(emb[:, t0:t1, :].rearrange(flat)),
                                     ACT.Copy).then_inc(first_copied, 1)
                act.wait_ge(rest_done, CHUNKS * f + c + 1)
                nc.scalar.activation(nat[b][:, 1, t0:t1, :].rearrange(flat), upper(rest[c % 2][:, :]),
                                     ACT.Copy).then_inc(mid_copied, 1)

            def copy_out(f, b, c):
                for a in range(PARTS):
                    m = PARTS * c + a
                    act.wait_ge(et_full, PARTS * CHUNKS * f + m + 1)
                    nc.scalar.activation(emb_t[b][:, a, CHUNK * c * P:CHUNK * (c + 1) * P],
                                         et_ps[m % 2][:, 0:CHUNK * P], ACT.Copy).then_inc(et_copied, 1)

            def body(i, b, scores=False):
                at[0] = 0
                q0 = RING * (i - FIRST_SCORE) if scores else 0
                gap = (lambda n: fill(q0, n)) if scores else (lambda n: None)
                has_front = not isinstance(i, int) or i < NG
                routed = active(i, 0) or active(i, 1)
                if isinstance(i, int) and i == 0:
                    for c in range(CHUNKS):
                        parts(i, b, c)
                        copy_out(i, b, c)
                    return
                if has_front:
                    if active(i, 2):
                        act.wait_ge(p_done[2], i - 2)
                        act.wait_ge(last_read, i - 2)
                    parts(i, b, 0)
                    copy_out(i, b, 0)
                gap(FILL[0])
                if has_front:
                    parts(i, b, 1)
                gap(FILL[1])
                if has_front:
                    copy_out(i, b, 1)
                gap(FILL[2])
                if has_front:
                    parts(i, b, 2)
                gap(FILL[3])
                if has_front:
                    copy_out(i, b, 2)
                gap(FILL[4])
                if has_front:
                    parts(i, b, 3)
                if active(i, 2):
                    act.wait_ge(att_less_ready, i - 2)
                    nc.scalar.activation(att_ex[:, :, :], att_less[:, :, :], ACT.Exp).then_inc(att_exp_done, 1)
                if has_front:
                    copy_out(i, b, 3)
                    parts(i, b, 4)
                    copy_out(i, b, 4)
                gap(3)
                if routed:
                    act.wait_ge(less_ready, i)
                    nc.scalar.activation(ex[:, :, :], less[:, :, :], ACT.Exp).then_inc(exp_done, 1)
                gap(FILL[5] - 3)

            for i in range(BUFS):
                body(i, i)
            with act.Fori(1, FIRST_SCORE // BUFS) as j:
                for b in range(BUFS):
                    body(BUFS * j + b, b)
            with act.Fori(FIRST_SCORE // BUFS, NG // BUFS) as j:
                for b in range(BUFS):
                    body(BUFS * j + b, b, scores=True)
            for i in range(NG // BUFS * BUFS, LAST_BODY + 1):
                body(i, i % BUFS, scores=True)

            with act.Fori(IN_BODIES, 2 * NPIECE) as q:
                for m in range(MT):
                    for c in range(SPLITS):
                        copy_scores(q, m, c)

        @block.vector
        def _(dve):
            steps = [0]
            base = [0]

            def note(ins):
                steps[0] += 1
                ins.then_inc(dve_step, 1)
                return steps[0]

            def after(number):
                dve.wait_ge(dve_step, base[0] + number)

            def step(ins):
                after(note(ins))

            def tt(o, a, b, op):
                return nc.vector.tensor_tensor(o, a, b, op)

            def less_part(o, a):
                return tt(o, a, upper(a), ALU.subtract)

            dve.wait_ge(loaded, 16 * (LOADS - 1))
            dve.wait_ge(made, MADE_BY_POOL)
            scratch = tab[2][:, 0:K * HID]
            for words, to in ((tab[0][:, 0:K * HID], w_sb), (tab[1][:, 0:K * HID], wt_sb)):
                o = [to[:, a, :, :].rearrange("p k n -> p (k n)") for a in range(PARTS)]
                step(nc.vector.tensor_copy(o[0], upper(words)))
                step(less_part(scratch, words))
                step(nc.vector.tensor_copy(o[1], upper(scratch)))
                step(less_part(o[2], scratch))
            step(nc.vector.memset(brow[:, :], 0.0))
            words = tab[3][0:PARTS, 0:K * HID]
            left = scratch[0:PARTS, :]
            one, two = (r[0:PARTS, 0:K * HID] for r in rest)
            step(less_part(left, words))
            step(nc.vector.tensor_scalar(one, upper(words), ident_f[0:PARTS, 0:1], None, ALU.mult))
            step(nc.vector.scalar_tensor_tensor(two, upper(left), ident_f[0:PARTS, 1:2], one, ALU.mult, ALU.add))
            step(less_part(one, left))
            step(nc.vector.scalar_tensor_tensor(brow[0:PARTS, :], one, ident_f[0:PARTS, 2:3], two, ALU.mult, ALU.add))
            step(nc.vector.tensor_copy(ident_b[:, :], ident_f[:, :]))
            step(nc.vector.tensor_scalar(quarter[:, :, :], slot_sb[:, :, 0:SK:K], 1.0 / K, None, ALU.mult))
            for t in (mask[BUFS - 1][:, :, :], nonzero[:, :], qb[:, :, :, :, :], summed[:, :, :, :], c_sb[:, :, :, :], before[:, :, :],
                      l_ps[:, :, :], pa_ps[:, :]):
                step(nc.vector.memset(t, 0.0))
            step(nc.vector.memset(pooled[:, :, :, :], 0.0))
            step(nc.vector.memset(pooled[:, 0, 1, 0:GK], float(SEQ) / K))
            nc.vector.memset(s_sb[:, :], 0.0).then_inc(made, 1)
            dve.wait_ge(made, MADE_BY_POOL + 1)

            def rests(f, b, c):
                dve.wait_ge(gathered[c], 16 * CHUNK * (f + 1))
                if not (isinstance(f, int) and f == 0 and c < 2):
                    if c == 0:
                        dve.wait_ge(mid_copied, CHUNKS * f)
                    elif c > 1:
                        dve.wait_ge(mid_copied, CHUNKS * f + c - 1)
                e = emb[:, CHUNK * c:CHUNK * (c + 1), :].rearrange("p t n -> p (t n)")
                less_part(rest[c % 2][:, :], e).then_inc(rest_done, 1)

            def lows(f, b, c):
                dve.wait_ge(rest_done, CHUNKS * f + c + 1)
                if c == 0 and active(f, 2):
                    dve.wait_ge(p_done[2], f - 2)
                less_part(nat[b][:, 2, CHUNK * c:CHUNK * (c + 1), :].rearrange("p t n -> p (t n)"),
                          rest[c % 2][:, :]).then_inc(low_done, 1)

            def make_mask(f, b, use):
                dve.wait_ge(idx_in[b], 16 * (use + 1))
                nc.vector.tensor_scalar(nonzero[:, 0:TILES], idx[b][:, :].bitcast(I32), 0.0, None, ALU.not_equal)\
                  .then_inc(nz_done, 1)
                dve.wait_ge(nz_done, f + 1)
                tt(mask[b][:, :, :], slot_sb[:, :, :], nonzero[:, :].unsqueeze(2).to_broadcast([P, PADT, SK]), ALU.mult)

            def pool_parts(i):
                lanes = [(2, pb_ps), (1, pa_ps)]
                for lane, bank in lanes:
                    if active(i, lane):
                        dve.wait_ge(p_done[lane], i - lane)
                        if lane == 1 and active(i, 0):
                            dve.wait_ge(p_done[0], i)
                        view = bank[:, 0:2 * PW].rearrange("p (s a x) -> p s x a", s=2, a=PARTS)[:, :, 0:GK, :]
                        step(nc.vector.tensor_reduce(pooled[:, 0, :, lane * GK:(lane + 1) * GK], view, AX.X, ALU.add))
                if active(i, 0):
                    dve.wait_ge(p_done[0], i)
                    step(nc.vector.tensor_copy(pooled[:, 0, 0, 0:GK].rearrange("p (b k) -> p b k", k=K),
                                               first_out[:, 0:GROUP].unsqueeze(2).to_broadcast([P, GROUP, K])))
                w3 = [pooled[:, a, :, :].rearrange("p s x -> p (s x)") for a in range(PARTS)]
                step(less_part(w3[1], w3[0]))
                less_part(w3[2], w3[1]).then_inc(pooled_ready, 1)

            def squares(i):
                dve.wait_ge(s_done, i)
                for u in range(2):
                    to = s_sb[:, :].rearrange("p (x u k) -> p u k x", u=2, k=2)[:, u, :, :]
                    step(nc.vector.tensor_reduce(to, s_out[:, u, :, :, :].rearrange("p k a x -> p k x a"), AX.X, ALU.add))
                tt(sq[:, :], s_sb[:, :], s_sb[:, :], ALU.mult).then_inc(sq_ready, 1)

            def factors(i):
                n2, n2p1, g1, ta, tb, r, f, nn = (t[0:NORM_ROWS, :] for t in rs)
                dve.wait_ge(n_done, i)
                g = guess[0:NORM_ROWS, :]
                nc.vector.tensor_copy(n2, norm_out)
                step(nc.vector.tensor_scalar(g, norm_out.bitcast(I32), -0.5, RSQRT_MAGIC, ALU.mult, ALU.add))
                r0 = g.bitcast(F32)
                for newton in range(3):
                    step(tt(ta, n2, r0, ALU.mult))
                    step(nc.vector.scalar_tensor_tensor(tb, ta, -0.5, r0, ALU.mult, ALU.mult))
                    o = (r, g1, nn)[newton]
                    step(nc.vector.scalar_tensor_tensor(o, tb, 1.5, r0 if newton < 2 else ta, ALU.add, ALU.mult))
                    r0 = o
                step(nc.vector.tensor_scalar(n2p1, n2, 1.0, None, ALU.add))
                step(nc.vector.scalar_tensor_tensor(ta, nn, 1e-12, n2p1, ALU.add, ALU.mult))
                step(nc.vector.reciprocal(tb, ta))
                step(tt(f, n2, tb, ALU.mult))
                nc.vector.tensor_scalar(diag[0:NORM_ROWS, 0, :], ident_f[0:NORM_ROWS, 0:NORM_ROWS], f[:, 0:1], None, ALU.mult)
                nc.vector.tensor_scalar(diag[0:NORM_ROWS, 1, :], ident_f[0:NORM_ROWS, 0:NORM_ROWS], f[:, 1:2], None,
                                        ALU.mult).then_inc(diag_ready, 1)

            def capsules(i):
                dve.wait_ge(f_done, i)
                step(tt(v_sb[:, 0, :], s_sb[:, :], factor_out, ALU.mult))
                if active(i, 0) or active(i, 1):
                    two = 2 * GK
                    step(less_part(v_sb[:, 1, 0:two], v_sb[:, 0, 0:two]))
                    less_part(v_sb[:, 2, 0:two], v_sb[:, 1, 0:two]).then_inc(v_ready, 1)
                    for lane in range(2):
                        tt(qb[:, 0, 1, lane, 0:GK].rearrange("p (b k) -> p b k", k=K),
                           v_sb[:, 0, lane * GK:(lane + 1) * GK].rearrange("p (b k) -> p b k", k=K),
                           bias_sb[:, :].unsqueeze(1).to_broadcast([P, GROUP, K]), ALU.mult)
                if active(i, 2):
                    tt(att[:, :, :], v_sb[:, 0, 2 * GK:3 * GK].rearrange("p (b k) -> p b k", k=K),
                       last_t[:, :].unsqueeze(2).to_broadcast([P, GROUP, K]), ALU.mult).then_inc(prod_ready, 1)

            def back_parts(i):
                dve.wait_ge(q_done, i)
                for u in range(2):
                    for lane in range(2):
                        to = qb[:, 0, 0, lane, 0:GK].rearrange("p (x u k) -> p u k x", u=2, k=2)[:, u, :, :]
                        src = q_out[:, u, :, :, lane * GROUP:(lane + 1) * GROUP].rearrange("p k a x -> p k x a")
                        ins = nc.vector.tensor_reduce(to, src, AX.X, ALU.add)
                step(ins)
                q = [qb[:, a, :, :, :].rearrange("p s l x -> p (s l x)") for a in range(PARTS)]
                step(less_part(q[1], q[0]))
                less_part(q[2], q[1]).then_inc(qb_ready, 1)

            def attention_exponents(i):
                dve.wait_ge(a_done, i - 2)
                step(nc.vector.tensor_copy(att_sum3, att_out.rearrange("p (b k) -> p b k", k=K)))
                step(nc.vector.tensor_reduce(att_top[:, :], att_sum3, AX.X, ALU.max))
                tt(att_less[:, :, :], att_sum3, att_top[:, :].unsqueeze(2).to_broadcast([P, GROUP, K]), ALU.subtract)\
                    .then_inc(att_less_ready, 1)

            att_sum3 = att[:, :, :]

            def finish(i):
                dve.wait_ge(att_exp_done, i - 2)
                v3 = v_sb[:, 0, 2 * GK:3 * GK].rearrange("p (b k) -> p b k", k=K)
                nc.vector.tensor_reduce(att_total[:, :], att_ex[:, :, :], AX.X, ALU.add)
                step(tt(att[:, :, :], att_ex[:, :, :], v3, ALU.mult))
                nc.vector.reciprocal(att_top[:, :], att_total[:, :])
                step(nc.vector.tensor_reduce(att_sum[:, :], att[:, :, :], AX.X, ALU.add))
                tt(final_t[:, bass.ds((i - 3) * GROUP, GROUP)], att_sum[:, :], att_top[:, :], ALU.mult)\
                    .then_inc(final_done, 1)

            def take_logits(i, lane, u):
                dve.wait_ge(l_done[lane][u], i - lane)
                tiles = HALF if u == 0 else TILES - HALF
                ins = nc.vector.tensor_reduce(
                    summed[:, lane, HALF * u:HALF * u + tiles, :],
                    l_ps[:, u, 0:tiles * LW].rearrange("p (t a x) -> p t x a", t=tiles, a=PARTS), AX.X, ALU.add)
                if lane == 1:
                    ins.then_inc(l_read[u], 1)
                return ins

            def weights(i, b):
                flat = "p t x -> p (t x)"
                for lane in range(2):
                    ins = tt(masked[:, lane, :, :].rearrange(flat), summed[:, lane, :, :].rearrange(flat),
                             mask[(b - 1 - lane) % BUFS][:, :, :].rearrange(flat), ALU.mult)
                step(ins)
                both = masked[:, :, :, :].rearrange("p l t x -> p (l t) x")
                step(tt(logit[:, :, :, :].rearrange("p l t k -> p (l t) k"), both[:, :, 0:K], both[:, :, K:SK], ALU.add))
                step(tt(logit[:, 1, :, :], logit[:, 1, :, :], before[:, :, :], ALU.add))
                x = logit[:, :, :, :].rearrange("p l t k -> p (l t) k")
                step(nc.vector.tensor_reduce(top[:, :], x, AX.X, ALU.max))
                tt(less[:, :, :], x, top[:, :].unsqueeze(2).to_broadcast([P, 2 * PADT, K]), ALU.subtract)\
                    .then_inc(less_ready, 1)
                nc.vector.tensor_copy(before[:, :, :], logit[:, 0, :, :])
                dve.wait_ge(exp_done, i)
                totalled = note(nc.vector.tensor_reduce(total[:, :], ex[:, :, :], AX.X, ALU.add))
                for lane in range(2):
                    t0, t1 = lane * PADT, (lane + 1) * PADT
                    ins = tt(own[:, t0:t1, :].rearrange("p t (s k) -> p t s k", k=K),
                             slot_sb[:, :, :].rearrange("p t (s k) -> p t s k", k=K),
                             ex[:, t0:t1, :].unsqueeze(2).to_broadcast([P, PADT, SLOTS, K]), ALU.mult)
                after(totalled)
                step(nc.vector.reciprocal(inv[:, :], total[:, :]))
                step(tt(c_sb[:, :, 0, :].rearrange("p l (t x) -> p l t x", x=SK),
                        own[:, :, :].rearrange("p (l t) x -> p l t x", l=2),
                        inv[:, :].rearrange("p (l t) -> p l t", l=2).unsqueeze(3).to_broadcast([P, 2, PADT, SK]), ALU.mult))
                step(less_part(c_sb[:, :, 1, :], c_sb[:, :, 0, :]))
                less_part(c_sb[:, :, 2, :], c_sb[:, :, 1, :]).then_inc(c_ready, 1)

            def last_items(i, b):
                dve.wait_ge(et_copied, PARTS * CHUNKS * (i - 1))
                nc.vector.tensor_reduce(
                    last_t[:, :], emb_t[(b - 2) % BUFS][:, :, SEQ - 1:TILES * P:SEQ].rearrange("p a b -> p b a"),
                    AX.X, ALU.add).then_inc(last_read, 1)

            def body(i, b, use, count):
                base[0], steps[0] = count, 0
                has_front = not isinstance(i, int) or i < NG
                routed = active(i, 0) or active(i, 1)
                if has_front:
                    make_mask(i, b, use)
                    rests(i, b, 0)
                    lows(i, b, 0)
                if isinstance(i, int) and i == 0:
                    for c in range(1, CHUNKS):
                        rests(i, b, c)
                        lows(i, b, c)
                    return steps[0]
                pool_parts(i)
                if has_front:
                    rests(i, b, 1)
                squares(i)
                if has_front:
                    lows(i, b, 1)
                factors(i)
                if has_front:
                    rests(i, b, 2)
                capsules(i)
                if has_front:
                    lows(i, b, 2)
                if routed:
                    back_parts(i)
                if has_front:
                    rests(i, b, 3)
                    lows(i, b, 3)
                if active(i, 2):
                    attention_exponents(i)
                if active(i, 1):
                    for u in range(2):
                        take_logits(i, 1, u)
                if active(i, 2):
                    finish(i)
                if active(i, 1):
                    last_items(i, b)
                if has_front:
                    rests(i, b, 4)
                    lows(i, b, 4)
                if active(i, 0):
                    for u in range(2):
                        ins = take_logits(i, 0, u)
                    step(ins)
                if routed:
                    weights(i, b)
                return steps[0]

            done = steps[0]
            for i in range(BUFS):
                done += body(i, i, 0, done)
            for first, end in ((1, FIRST_SCORE // BUFS), (FIRST_SCORE // BUFS, NG // BUFS)):
                with dve.Fori(first, end) as j:
                    for b in range(BUFS):
                        n = body(BUFS * j + b, b, j, done - first * BUFS * BODY_STEPS + BODY_STEPS * (BUFS * j + b))
                        assert n == BODY_STEPS, n
                done += BODY_STEPS * BUFS * (end - first)
            for i in range(NG // BUFS * BUFS, LAST_BODY + 1):
                done += body(i, i % BUFS, i // BUFS, done)


BODY_STEPS = 37


def kernel(r_seq, L0_rec_emb_table, L0_rec_s_w, L0_rec_s_b):
    import concourse.bacc as bacc
    from concourse.bass_utils import run_bass_kernel_spmd

    r_seq, table, w, b = (np.asarray(x) for x in (r_seq, L0_rec_emb_table, L0_rec_s_w, L0_rec_s_b))
    position = np.arange(TILES * P).reshape(TILES, P).T
    slot = np.zeros((P, PADT, SLOTS, K), np.float32)
    for s in range(SLOTS):
        slot[:, :TILES, s, :] = (position // SEQ == np.array(FIRST_SEQ) + s)[:, :, None]
    arrays = {
        "index": np.ascontiguousarray(r_seq.reshape(NG, TILES, P).transpose(0, 2, 1)).view(np.uint32),
        "table": np.ascontiguousarray(table),
        "table_t": np.ascontiguousarray(table.T),
        "w": np.ascontiguousarray(w),
        "w_t": np.ascontiguousarray(w.reshape(HID, K, HID).transpose(2, 1, 0).reshape(HID, K * HID)),
        "bias": np.ascontiguousarray(b.reshape(K, HID).T),
        "bias_rows": np.ascontiguousarray(np.broadcast_to(b, (PARTS, K * HID))),
        "ident": np.eye(P, dtype=np.float32),
        "slot_mask": slot.reshape(P, -1),
    }
    nc = bacc.Bacc("TRN2", target_bir_lowering=False, num_devices=1)
    args = [nc.dram_tensor(n, a.shape, mybir.dt.from_np(a.dtype), kind="ExternalInput").ap() for n, a in arrays.items()]
    out = nc.dram_tensor("scores", (BATCH, ITEMS), F32, kind="ExternalOutput").ap()
    build(nc, *args, out)
    r = run_bass_kernel_spmd(nc, [arrays], core_ids=[0])
    return r.results[0]["scores"]
```

```python
from contextlib import ExitStack

import numpy as np

import concourse.bass as bass
from concourse import mybir

F32 = mybir.dt.float32
BF16 = mybir.dt.bfloat16
I32 = mybir.dt.int32
U32 = mybir.dt.uint32
ALU = mybir.AluOpType
ACT = mybir.ActivationFunctionType
AX = mybir.AxisListType

P = 128
BATCH, SEQ, K, HID, ITEMS = 1024, 200, 4, 128, 100000
GROUP = 16
TILES = GROUP * SEQ // P
NG = BATCH // GROUP
PADT = TILES + 1
HALF = PADT // 2
PADG = GROUP + 1
SLOTS = 2
PARTS = 3
LANES = 3
CHUNK = 5
CHUNKS = TILES // CHUNK
GK = GROUP * K
SK = SLOTS * K
LW = PARTS * SK
PW = PARTS * PADG * K
NORM_ROWS = LANES * GK // 2
BUFS = 3
AHEAD = 2
RSQRT_MAGIC = 1595932665.0
RSQRT_C0, RSQRT_C1 = 0.703952253, 0.703952253 * 2.38924456

FIRST_TILE = (0, 2)
SHARE_TILES = (2, BATCH // P - 2)
PIECE = 1000
COLS = 500
SPLITS = PIECE // COLS
NPIECE = ITEMS // PIECE
RING = 2
PER_PIECE = [n * SPLITS for n in SHARE_TILES]
BEFORE = (0, NPIECE * PER_PIECE[0])
FIRST_SCORE = 21
LAST_BODY = NG + LANES - 1
FILL = (0, 1, 2, 2, 1, 1, 1)
BEFORE_EXP = 1
assert all(n % 2 == 0 for n in PER_PIECE) and PER_PIECE[1] % 4 == 0 and SPLITS == 2
assert sum(FILL) == RING * PER_PIECE[0] and FIRST_SCORE % BUFS == 0 and NPIECE % RING == 0
IN_BODIES = (LAST_BODY - FIRST_SCORE + 1) * RING

FIRST_SEQ = [P * t // SEQ for t in range(TILES)]


def upper(ap):
    names = " ".join("abcd"[: len(ap.shape) - 2])
    v = ap.bitcast(BF16)
    return v.rearrange(f"p {names} (n two) -> p {names} n two", two=2)[..., 1]


def build(nc, index, table, table_t, w, w_t, bias, bias_rows, ident, slot_mask, out):
    ctx = ExitStack()
    with ctx:
        def sb(name, shape, dt=F32):
            return ctx.enter_context(nc.sbuf_tensor(name, shape, dt))

        def ps(name, shape, dt=F32):
            return ctx.enter_context(nc.psum_tensor(name, shape, dt))

        def sem(name):
            return ctx.enter_context(nc.semaphore(name))

        idx = [sb(f"idx{b}", [P, TILES], U32) for b in range(BUFS)]
        emb = sb("emb", [P, TILES, HID])
        rest = [sb(f"rest{r}", [P, CHUNK * HID]) for r in range(2)]
        nat = [sb(f"nat{b}", [P, PARTS, TILES, HID], BF16) for b in range(BUFS)]
        emb_t = [sb(f"emb_t{b}", [P, PARTS, TILES * P], BF16) for b in range(BUFS)]
        mask = [sb(f"mask{b}", [P, PADT, SK]) for b in range(BUFS)]
        w_sb = sb("w_sb", [P, PARTS, K, HID], BF16)
        wt_sb = sb("wt_sb", [P, PARTS, K, HID], BF16)
        bias_sb = sb("bias_sb", [P, K])
        brow = sb("brow", [P, K * HID], BF16)
        ident_f = sb("ident_f", [P, P])
        ident_b = sb("ident_b", [P, P], BF16)
        ones_b = sb("ones_b", [P, P], BF16)
        ones_f = sb("ones_f", [P, P])
        zeros_b = sb("zeros_b", [P, 2 * PW], BF16)
        slot_sb = sb("slot_sb", [P, PADT, SK])
        quarter = sb("quarter", [P, PADT, SLOTS], BF16)
        nonzero = sb("nonzero", [P, PADT])
        pooled = sb("pooled", [P, PARTS, 2, LANES * GK])
        s_sb = sb("s_sb", [P, LANES * GK])
        sq = sb("sq", [P, LANES * GK])
        rs = [sb(f"rs{i}", [P, 2]) for i in range(8)]
        guess = sb("guess", [P, 2], I32)
        diag = sb("diag", [P, 2, NORM_ROWS])
        v_sb = sb("v_sb", [P, PARTS, LANES * GK])
        qb = sb("qb", [P, PARTS, 2, 2, PADG * K])
        summed = sb("summed", [P, 2, PADT, SK])
        masked = sb("masked", [P, 2, PADT, SK])
        logit = sb("logit", [P, 2, PADT, K])
        before = sb("before", [P, PADT, K])
        top = sb("top", [P, 2 * PADT])
        less = sb("less", [P, 2 * PADT, K])
        ex = sb("ex", [P, 2 * PADT, K])
        share = sb("share", [P, 2 * PADT, K])
        total = sb("total", [P, 2 * PADT])
        inv = sb("inv", [P, 2 * PADT])
        c_sb = sb("c_sb", [P, 2, PARTS, PADT * SK])
        last_t = sb("last_t", [P, GROUP])
        att = sb("att", [P, GROUP, K])
        att_top = sb("att_top", [P, GROUP])
        att_less = sb("att_less", [P, GROUP, K])
        att_ex = sb("att_ex", [P, GROUP, K])
        att_total = sb("att_total", [P, GROUP])
        att_sum = sb("att_sum", [P, GROUP])
        final_t = sb("final_t", [P, BATCH])
        tab = [sb(f"tab{r}", [P, PIECE]) for r in range(RING)]
        score_sb = [sb(f"score{m}", [P, PIECE]) for m in range(3)]
        emb_words = emb[:, :, :].rearrange("p t n -> p (t n)")
        score = [t[:, :] for t in score_sb] + [emb_words[:, m * PIECE:(m + 1) * PIECE] for m in range(3)]

        et_ps = [ps(f"et_ps{i}", [P, 2 * 512], BF16) for i in range(2)]
        l_ps = ps("l_ps", [P, 2, 512])
        pa_ps = ps("pa_ps", [P, 512])
        pb_ps = ps("pb_ps", [P, 512])
        sc_ps = [ps(f"sc_ps{i}", [P, 512]) for i in range(2)]
        banks = (sc_ps, sc_ps + [pa_ps, pb_ps])
        LB = LANES * GROUP
        s_out = l_ps[:, :, 0:2 * PARTS * LB].rearrange("p u (k a x) -> p u k a x", k=2, a=PARTS)
        q_out = l_ps[:, :, 0:2 * PARTS * 2 * GROUP].rearrange("p u (k a x) -> p u k a x", k=2, a=PARTS)
        first_out = pb_ps[:, 2 * PW:2 * PW + PADG]
        factor_out = pa_ps[:, 0:LANES * GK]
        norm_out = pb_ps[0:NORM_ROWS, 0:2]
        att_out = pb_ps[:, 64:64 + GK]

        loaded = sem("loaded")
        made = sem("made")
        idx_in = [sem(f"idx_in{b}") for b in range(BUFS)]
        gathered = [sem(f"gathered{c}") for c in range(CHUNKS)]
        nz_done = sem("nz_done")
        first_copied = sem("first_copied")
        rest_done = sem("rest_done")
        mid_copied = sem("mid_copied")
        low_done = sem("low_done")
        et_full = sem("et_full")
        et_copied = sem("et_copied")
        p_done = [sem(f"p_done{n}") for n in range(LANES)]
        pooled_ready = sem("pooled_ready")
        s_done = sem("s_done")
        sq_ready = sem("sq_ready")
        n_done = sem("n_done")
        diag_ready = sem("diag_ready")
        f_done = sem("f_done")
        v_ready = sem("v_ready")
        q_done = sem("q_done")
        qb_ready = [sem(f"qb_ready{n}") for n in range(2)]
        l_done = [[sem(f"l_done{n}_{u}") for u in range(2)] for n in range(2)]
        l_read = [sem(f"l_read{u}") for u in range(2)]
        less_ready = [sem(f"less_ready{n}") for n in range(2)]
        exp_done = [sem(f"exp_done{n}") for n in range(2)]
        c_ready = [sem(f"c_ready{n}") for n in range(2)]
        prod_ready = sem("prod_ready")
        a_done = sem("a_done")
        att_less_ready = sem("att_less_ready")
        att_exp_done = sem("att_exp_done")
        last_read = sem("last_read")
        final_done = sem("final_done")
        dve_step = sem("dve_step")
        tab_in = [sem(f"tab_in{r}") for r in range(RING)]
        scored = sem("scored")
        copied = sem("copied")
        stored = [sem(f"stored{m}") for m in range(SHARE_TILES[1])]

        LOADS, MADE_BY_POOL = 7, 3
        block = ctx.enter_context(nc.Block())

        def active(i, lane):
            return not isinstance(i, int) or 0 <= i - 1 - lane < NG

        @block.sync
        def _(sp):
            sp.dma_start(tab[0][:, 0:K * HID], w).then_inc(loaded, 16)
            sp.dma_start(tab[1][:, 0:K * HID], w_t).then_inc(loaded, 16)
            sp.dma_start(bias_sb[:, :], bias).then_inc(loaded, 16)
            sp.dma_start(score_sb[0][0:PARTS, 0:K * HID], bias_rows).then_inc(loaded, 16)
            sp.dma_start(ident_f[:, :], ident).then_inc(loaded, 16)
            sp.dma_start(slot_sb[:, :, :], slot_mask.rearrange("p (t x) -> p t x", x=SK)).then_inc(loaded, 16)
            for b in range(BUFS):
                sp.dma_start(idx[b][:, :], index[b, :, :]).then_inc(idx_in[b], 16)

            def indices(f, b):
                sp.compute_val(16 * CHUNK * (f - BUFS + 1))
                sp.compute_val(f - BUFS + 1)
                sp.wait_ge(loaded, 16 * (LOADS - 1))
                for c in range(CHUNKS):
                    sp.wait_ge(gathered[c], 16 * CHUNK * (f - BUFS + 1))
                sp.wait_ge(nz_done, f - BUFS + 1)
                sp.dma_start(idx[b][:, :], index[f, :, :]).then_inc(idx_in[b], 16)

            def load(q, r):
                sp.dma_start(tab[r][:, :], table_t[:, bass.ds(q * PIECE, PIECE)]).then_inc(tab_in[r], 16)

            def stores(q, share):
                for m in range(SHARE_TILES[share]):
                    row = (FIRST_TILE[share] + m) * P
                    done = PER_PIECE[share] * q + SPLITS * (m + 1) + BEFORE[share]
                    sp.compute_val(done)
                    sp.wait_ge(loaded, 16 * (LOADS - 1))
                    sp.wait_ge(copied, done)
                    sp.dma_start(out[row:row + P, bass.ds(q * PIECE, PIECE)], score[m]).then_inc(stored[m], 16)

            sp.wait_ge(made, MADE_BY_POOL + 1)
            for r in range(RING):
                load(r, r)

            def of_body(i, b):
                if not isinstance(i, int) or i + AHEAD < NG:
                    indices(i + AHEAD, (b + AHEAD) % BUFS)
                for r in range(RING):
                    q = RING * (i - FIRST_SCORE) + r
                    stores(q, 0)
                    load(q + RING, r)

            with sp.Fori(1, FIRST_SCORE // BUFS) as j:
                for b in range(BUFS):
                    indices(BUFS * j + b, b)
            for f in range(FIRST_SCORE, FIRST_SCORE + AHEAD):
                indices(f, f % BUFS)
            looped = (NG - AHEAD) // BUFS
            with sp.Fori(FIRST_SCORE // BUFS, looped) as j:
                for b in range(BUFS):
                    of_body(BUFS * j + b, b)
            for i in range(BUFS * looped, LAST_BODY):
                of_body(i, i % BUFS)
            for q in range(IN_BODIES - RING, NPIECE):
                stores(q, 0)
                load((q + RING) % NPIECE, q % RING)
            with sp.Fori(0, NPIECE // RING - 1) as j:
                for r in range(RING):
                    stores(RING * j + r, 1)
                    load(RING * (j + 1) + r, r)
            for q in range(NPIECE - RING, NPIECE):
                stores(q, 1)
            for m in range(SHARE_TILES[1]):
                sp.wait_ge(stored[m], 16 * NPIECE * (2 if m < SHARE_TILES[0] else 1))

        @block.gpsimd
        def _(pool):
            pool.memset(ones_b[:, :], 1.0).then_inc(made, 1)
            pool.memset(ones_f[:, :], 1.0).then_inc(made, 1)
            pool.memset(zeros_b[:, :], 0.0).then_inc(made, 1)

            def gather(f, b, use):
                for c in range(CHUNKS):
                    if not (isinstance(f, int) and f == 0):
                        pool.compute_val(CHUNKS * (f - 1) + c + 1)
                        pool.compute_val(16 * (use + 1))
                        pool.wait_ge(loaded, 16)
                        pool.wait_ge(first_copied, CHUNKS * (f - 1) + c + 1)
                        pool.wait_ge(rest_done, CHUNKS * (f - 1) + c + 1)
                    if c == 0:
                        pool.wait_ge(idx_in[b], 16 * (use + 1))
                    for t in range(CHUNK * c, CHUNK * (c + 1)):
                        pool.indirect_dma_start(
                            emb[:, t, :], None, table, bass.IndirectOffsetOnAxis(ap=idx[b][:, t:t + 1], axis=0),
                        ).then_inc(gathered[c], 16)

            for f in range(BUFS):
                gather(f, f, 0)
            with pool.Fori(1, NG // BUFS) as j:
                for b in range(BUFS):
                    gather(BUFS * j + b, b, j)
            gather(NG - 1, (NG - 1) % BUFS, (NG - 1) // BUFS)

        @block.tensor
        def _(pe):
            at = [0]

            def fill(q0, use, count):
                for s in range(at[0], at[0] + count):
                    p, s = divmod(s, PER_PIECE[0])
                    product(q0 + p, p, use, 0, *divmod(s, SPLITS))
                at[0] += count

            def product(q, r, use, share, m, c):
                if m == 0 and c == 0:
                    pe.wait_ge(tab_in[r], 16 * (use + 1))
                s = BEFORE[share] + PER_PIECE[share] * q + SPLITS * m + c
                n = len(banks[share])
                if not (isinstance(s, int) and s < n):
                    pe.wait_ge(copied, s - n + 1)
                row = (FIRST_TILE[share] + m) * P
                nc.tensor.matmul(banks[share][(SPLITS * m + c) % n][:, 0:COLS], final_t[:, row:row + P],
                                 tab[r][:, c * COLS:(c + 1) * COLS], start=True, stop=True).then_inc(scored, 1)

            def front(f, b, c, parts=range(PARTS)):
                for a in parts:
                    ready = (first_copied, mid_copied, low_done)[a]
                    pe.wait_ge(ready, CHUNKS * f + c + 1)
                    m = PARTS * c + a
                    if m >= 2:
                        pe.wait_ge(et_copied, PARTS * CHUNKS * f + m - 1)
                    elif m == 0 and not (isinstance(f, int) and f == 0):
                        pe.wait_ge(et_copied, PARTS * CHUNKS * f)
                    for n in range(CHUNK):
                        last = nc.tensor.transpose(et_ps[m % 2][:, n * P:(n + 1) * P],
                                                   nat[b][:, a, CHUNK * c + n, :], ident_b[:, :])
                    last.then_inc(et_full, 1)

            def sum_first(b):
                nc.tensor.matmul(first_out, ones_b[:, :], zeros_b[:, 0:PADG], start=True, stop=False)
                for t in range(TILES):
                    x = FIRST_SEQ[t]
                    for a in range(PARTS):
                        last = nc.tensor.matmul(first_out[:, x:x + SLOTS], nat[b][:, a, t, :], quarter[:, t, :],
                                                start=False, stop=(t == TILES - 1 and a == PARTS - 1))
                last.then_inc(p_done[0], 1)

            def sum_weighted(b, lane, bank):
                nc.tensor.matmul(bank[:, 0:2 * PW], ones_b[:, :], zeros_b[:, :], start=True, stop=False)
                sums, counts = (bank[:, s * PW:(s + 1) * PW].rearrange("p (a x) -> p a x", a=PARTS) for s in range(2))
                for t in range(TILES):
                    x = FIRST_SEQ[t] * K
                    c3 = upper(c_sb[:, lane - 1, :, t * SK:(t + 1) * SK])
                    for a in range(PARTS):
                        nc.tensor.matmul(sums[:, :, x:x + SK], nat[b][:, a, t, :], c3, start=False, stop=False)
                    last = nc.tensor.matmul(counts[:, :, x:x + SK], ones_b[:, :], c3,
                                            start=False, stop=(t == TILES - 1))
                last.then_inc(p_done[lane], 1)

            def logits(b, lane, u):
                for t in range(HALF * u, min(HALF * (u + 1), TILES)):
                    x = FIRST_SEQ[t] * K
                    y = (t - HALF * u) * LW
                    to = l_ps[:, u, y:y + LW].rearrange("p (a x) -> p a x", a=PARTS)
                    own_q, own_b = (upper(qb[:, :, s, lane, x:x + SK]) for s in range(2))
                    nc.tensor.matmul(to, ones_b[:, :], own_b, start=True, stop=False)
                    for a in range(PARTS):
                        last = nc.tensor.matmul(to, emb_t[b][:, a, t * P:(t + 1) * P], own_q,
                                                start=False, stop=(a == PARTS - 1))
                last.then_inc(l_done[lane][u], 1)

            def body(i, b, loop=None, scores=False):
                at[0] = 0
                q0 = RING * (i - FIRST_SCORE) if scores else 0
                gap = (lambda n: fill(q0, i - FIRST_SCORE, FILL[n])) if scores else (lambda n: None)
                has_front = not isinstance(i, int) or i < NG
                group_buf = [(b - 1 - lane) % BUFS for lane in range(LANES)]
                if isinstance(i, int) and i == 0:
                    for c in range(CHUNKS):
                        front(i, b, c)
                    return
                if active(i, 0):
                    sum_first(group_buf[0])
                if active(i, 2):
                    pe.wait_ge(c_ready[1], i - 2)
                    sum_weighted(group_buf[2], 2, pb_ps)
                gap(0)
                if active(i, 1):
                    pe.wait_ge(c_ready[0], i - 1)
                    sum_weighted(group_buf[1], 1, pa_ps)
                if has_front:
                    front(i, b, 0, range(2))
                gap(1)
                if has_front:
                    front(i, b, 0, range(2, 3))
                pe.wait_ge(pooled_ready, i)
                for k in range(K):
                    to = s_out[:, k // 2, k % 2, :, :]
                    part = [pooled[:, :, s, :].bitcast(BF16).rearrange("p a (x k two) -> p a x k two", k=K, two=2)
                            [:, :, :, k, 1] for s in range(2)]
                    for a in range(PARTS):
                        nc.tensor.matmul(to, w_sb[:, a, k, :], part[0], start=(a == 0), stop=False)
                    last = nc.tensor.matmul(to, brow[:, k * HID:(k + 1) * HID], part[1], start=False, stop=True)
                last.then_inc(s_done, 1)
                gap(2)
                pe.wait_ge(sq_ready, i)
                for n in range(2):
                    last = nc.tensor.matmul(norm_out[:, n:n + 1], sq[:, n * NORM_ROWS:(n + 1) * NORM_ROWS],
                                            ones_f[:, 0:1], start=True, stop=True)
                last.then_inc(n_done, 1)
                if has_front:
                    front(i, b, 1, range(2))
                gap(3)
                if has_front:
                    front(i, b, 1, range(2, 3))
                pe.wait_ge(diag_ready, i)
                for n in range(2):
                    last = nc.tensor.matmul(factor_out[:, n * NORM_ROWS:(n + 1) * NORM_ROWS],
                                            ones_f[0:NORM_ROWS, :], diag[0:NORM_ROWS, n, :], start=True, stop=True)
                last.then_inc(f_done, 1)
                gap(4)
                routed = active(i, 0) or active(i, 1)
                if routed:
                    pe.wait_ge(v_ready, i)
                    for k in range(K):
                        v3 = v_sb[:, :, 0:2 * GK].bitcast(BF16)\
                            .rearrange("p a (x k two) -> p a x k two", k=K, two=2)[:, :, :, k, 1]
                        for a in range(PARTS):
                            last = nc.tensor.matmul(q_out[:, k // 2, k % 2, :, :], wt_sb[:, a, k, :], v3,
                                                    start=(a == 0), stop=(a == PARTS - 1))
                    last.then_inc(q_done, 1)
                if has_front:
                    front(i, b, 2, range(1))
                gap(5)
                if has_front:
                    front(i, b, 2, range(1, 2))
                if active(i, 2):
                    pe.wait_ge(prod_ready, i - 2)
                    nc.tensor.matmul(att_out, ones_f[:, :], att[:, :, :].rearrange("p b k -> p (b k)"),
                                     start=True, stop=True).then_inc(a_done, 1)
                if active(i, 1):
                    pe.wait_ge(qb_ready[1], i - 1)
                    for u in range(2):
                        logits(group_buf[1], 1, u)
                if active(i, 0):
                    pe.wait_ge(qb_ready[0], i)
                if has_front:
                    front(i, b, 2, range(2, 3))
                for u in range(2):
                    if has_front:
                        front(i, b, 3, range(2 * u, 2 * u + 1))
                    if active(i, 0):
                        if active(i, 1):
                            pe.wait_ge(l_read[u], i - 1)
                        if u == 0:
                            pe.wait_ge(et_copied, PARTS * CHUNKS * i)
                        logits(group_buf[0], 0, u)
                    if has_front and u == 0:
                        front(i, b, 3, range(1, 2))
                if has_front:
                    front(i, b, 4)
                gap(6)

            pe.wait_ge(made, MADE_BY_POOL + 1)

            def run_pe():
                for i in range(BUFS):
                    body(i, i)
                with pe.Fori(1, FIRST_SCORE // BUFS) as j:
                    for b in range(BUFS):
                        body(BUFS * j + b, b)
                pe.wait_ge(final_done, SHARE_TILES[0] * P // GROUP)
                for i in range(FIRST_SCORE, FIRST_SCORE + BUFS):
                    body(i, i % BUFS, scores=True)
                with pe.Fori(FIRST_SCORE // BUFS + 1, NG // BUFS) as j:
                    for b in range(BUFS):
                        body(BUFS * j + b, b, scores=True)
                for i in range(NG // BUFS * BUFS, LAST_BODY + 1):
                    body(i, i % BUFS, scores=True)

            run_pe()

            def piece(q, r, use, share):
                for m in range(SHARE_TILES[share]):
                    for c in range(SPLITS):
                        product(q, r, use, share, m, c)

            for q in range(IN_BODIES, NPIECE):
                piece(q, q % RING, q // RING, 0)
            pe.wait_ge(final_done, NG)
            pe.wait_ge(copied, BEFORE[1])
            with pe.Fori(0, NPIECE // RING) as j:
                for r in range(RING):
                    piece(RING * j + r, r, j + NPIECE // RING, 1)

        @block.scalar
        def _(act):
            at = [0]

            def copy_scores(q, share, m, c):
                earlier = q + NPIECE if share == 1 and m < SHARE_TILES[0] else q
                if c == 0 and not (isinstance(earlier, int) and earlier == 0):
                    act.wait_ge(stored[m], 16 * earlier)
                act.wait_ge(scored, BEFORE[share] + PER_PIECE[share] * q + SPLITS * m + c + 1)
                bank = banks[share][(SPLITS * m + c) % len(banks[share])]
                nc.scalar.activation(score[m][:, c * COLS:(c + 1) * COLS], bank[:, 0:COLS], ACT.Copy)\
                    .then_inc(copied, 1)

            def piece(q, share):
                for m in range(SHARE_TILES[share]):
                    for c in range(SPLITS):
                        copy_scores(q, share, m, c)

            def fill(q0, count):
                for s in range(at[0], at[0] + count):
                    p, s = divmod(s, PER_PIECE[0])
                    copy_scores(q0 + p, 0, *divmod(s, SPLITS))
                at[0] += count

            def parts(f, b, c):
                t0, t1 = CHUNK * c, CHUNK * (c + 1)
                flat = "p t n -> p (t n)"
                act.wait_ge(gathered[c], 16 * CHUNK * (f + 1))
                nc.scalar.activation(nat[b][:, 0, t0:t1, :].rearrange(flat), upper(emb[:, t0:t1, :].rearrange(flat)),
                                     ACT.Copy).then_inc(first_copied, 1)
                act.wait_ge(rest_done, CHUNKS * f + c + 1)
                nc.scalar.activation(nat[b][:, 1, t0:t1, :].rearrange(flat), upper(rest[c % 2][:, :]),
                                     ACT.Copy).then_inc(mid_copied, 1)

            def copy_out(f, b, c, parts_copied=range(PARTS)):
                for a in parts_copied:
                    m = PARTS * c + a
                    act.wait_ge(et_full, PARTS * CHUNKS * f + m + 1)
                    nc.scalar.activation(emb_t[b][:, a, CHUNK * c * P:CHUNK * (c + 1) * P],
                                         et_ps[m % 2][:, 0:CHUNK * P], ACT.Copy).then_inc(et_copied, 1)

            def body(i, b, scores=False):
                at[0] = 0
                q0 = RING * (i - FIRST_SCORE) if scores else 0
                gap = (lambda n: fill(q0, n)) if scores else (lambda n: None)
                has_front = not isinstance(i, int) or i < NG
                routed = active(i, 0) or active(i, 1)
                if isinstance(i, int) and i == 0:
                    for c in range(CHUNKS):
                        parts(i, b, c)
                        copy_out(i, b, c)
                    return
                gap(FILL[0])
                if has_front:
                    if active(i, 2):
                        act.wait_ge(p_done[2], i - 2)
                        act.wait_ge(last_read, i - 2)
                    parts(i, b, 0)
                    copy_out(i, b, 0, range(2))
                gap(FILL[1])
                if has_front:
                    copy_out(i, b, 0, range(2, 3))
                    parts(i, b, 1)
                gap(FILL[2])
                if has_front:
                    copy_out(i, b, 1, range(2))
                gap(FILL[3])
                if has_front:
                    copy_out(i, b, 1, range(2, 3))
                    parts(i, b, 2)
                gap(FILL[4])
                if has_front:
                    copy_out(i, b, 2, range(1))
                gap(FILL[5])
                if has_front:
                    copy_out(i, b, 2, range(1, 2))
                    parts(i, b, 3)
                if active(i, 2):
                    act.wait_ge(att_less_ready, i - 2)
                    nc.scalar.activation(att_ex[:, :, :], att_less[:, :, :], ACT.Exp).then_inc(att_exp_done, 1)
                if has_front:
                    copy_out(i, b, 2, range(2, 3))
                    copy_out(i, b, 3, range(1))
                    parts(i, b, 4)
                if active(i, 1):
                    exponentials(i, 1)
                if has_front:
                    copy_out(i, b, 3, range(1, PARTS))
                    copy_out(i, b, 4)
                gap(BEFORE_EXP)
                if active(i, 0):
                    exponentials(i, 0)
                gap(FILL[6] - BEFORE_EXP)

            def exponentials(i, lane):
                act.wait_ge(less_ready[lane], i - lane)
                of = slice(lane * PADT, (lane + 1) * PADT)
                nc.scalar.activation(ex[:, of, :], less[:, of, :], ACT.Exp).then_inc(exp_done[lane], 1)

            for i in range(BUFS):
                body(i, i)
            with act.Fori(1, FIRST_SCORE // BUFS) as j:
                for b in range(BUFS):
                    body(BUFS * j + b, b)
            with act.Fori(FIRST_SCORE // BUFS, NG // BUFS) as j:
                for b in range(BUFS):
                    body(BUFS * j + b, b, scores=True)
            for i in range(NG // BUFS * BUFS, LAST_BODY + 1):
                body(i, i % BUFS, scores=True)

            with act.Fori(IN_BODIES, NPIECE) as q:
                piece(q, 0)
            piece(0, 1)
            with act.Fori(1, NPIECE) as q:
                piece(q, 1)

        @block.vector
        def _(dve):
            steps = [0]
            base = [0]

            def note(ins):
                steps[0] += 1
                ins.then_inc(dve_step, 1)
                return steps[0]

            def after(number):
                dve.wait_ge(dve_step, base[0] + number)

            def step(ins):
                after(note(ins))

            def tt(o, a, b, op):
                return nc.vector.tensor_tensor(o, a, b, op)

            def less_part(o, a):
                return tt(o, a, upper(a), ALU.subtract)

            dve.wait_ge(loaded, 16 * (LOADS - 1))
            dve.wait_ge(made, MADE_BY_POOL)
            scratch = score_sb[1][:, 0:K * HID]
            for words, to in ((tab[0][:, 0:K * HID], w_sb), (tab[1][:, 0:K * HID], wt_sb)):
                o = [to[:, a, :, :].rearrange("p k n -> p (k n)") for a in range(PARTS)]
                step(nc.vector.tensor_copy(o[0], upper(words)))
                step(less_part(scratch, words))
                step(nc.vector.tensor_copy(o[1], upper(scratch)))
                step(less_part(o[2], scratch))
            step(nc.vector.memset(brow[:, :], 0.0))
            words = score_sb[0][0:PARTS, 0:K * HID]
            left = scratch[0:PARTS, :]
            one, two = (r[0:PARTS, 0:K * HID] for r in rest)
            step(less_part(left, words))
            step(nc.vector.tensor_scalar(one, upper(words), ident_f[0:PARTS, 0:1], None, ALU.mult))
            step(nc.vector.scalar_tensor_tensor(two, upper(left), ident_f[0:PARTS, 1:2], one, ALU.mult, ALU.add))
            step(less_part(one, left))
            step(nc.vector.scalar_tensor_tensor(brow[0:PARTS, :], one, ident_f[0:PARTS, 2:3], two, ALU.mult, ALU.add))
            step(nc.vector.tensor_copy(ident_b[:, :], ident_f[:, :]))
            step(nc.vector.tensor_scalar(quarter[:, :, :], slot_sb[:, :, 0:SK:K], 1.0 / K, None, ALU.mult))
            for t in (mask[BUFS - 1][:, :, :], nonzero[:, :], qb[:, :, :, :, :], summed[:, :, :, :], c_sb[:, :, :, :], before[:, :, :],
                      l_ps[:, :, :], pa_ps[:, :]):
                step(nc.vector.memset(t, 0.0))
            step(nc.vector.memset(pooled[:, :, :, :], 0.0))
            step(nc.vector.memset(pooled[:, 0, 1, 0:GK], float(SEQ) / K))
            nc.vector.memset(s_sb[:, :], 0.0).then_inc(made, 1)
            dve.wait_ge(made, MADE_BY_POOL + 1)

            def rests(f, b, c):
                dve.wait_ge(gathered[c], 16 * CHUNK * (f + 1))
                if not (isinstance(f, int) and f == 0 and c < 2):
                    if c == 0:
                        dve.wait_ge(mid_copied, CHUNKS * f)
                        dve.wait_ge(low_done, CHUNKS * f)
                    elif c > 1:
                        dve.wait_ge(mid_copied, CHUNKS * f + c - 1)
                e = emb[:, CHUNK * c:CHUNK * (c + 1), :].rearrange("p t n -> p (t n)")
                less_part(rest[c % 2][:, :], e).then_inc(rest_done, 1)

            def lows(f, b, c):
                dve.wait_ge(rest_done, CHUNKS * f + c + 1)
                if c == 0 and active(f, 2):
                    dve.wait_ge(p_done[2], f - 2)
                less_part(nat[b][:, 2, CHUNK * c:CHUNK * (c + 1), :].rearrange("p t n -> p (t n)"),
                          rest[c % 2][:, :]).then_inc(low_done, 1)

            def make_mask(f, b, use):
                dve.wait_ge(idx_in[b], 16 * (use + 1))
                nc.vector.tensor_scalar(nonzero[:, 0:TILES], idx[b][:, :].bitcast(I32), 0.0, None, ALU.not_equal)\
                  .then_inc(nz_done, 1)
                rests(f, b, 0)
                dve.wait_ge(nz_done, f + 1)
                tt(mask[b][:, :, :], slot_sb[:, :, :], nonzero[:, :].unsqueeze(2).to_broadcast([P, PADT, SK]), ALU.mult)

            def split_sums(lanes):
                w3 = [pooled[:, a, :, :].rearrange("p s (l x) -> p s l x", l=LANES)[:, :, lanes, :] for a in range(PARTS)]
                step(less_part(w3[1], w3[0]))
                return less_part(w3[2], w3[1])

            def take_sums(i, lane, bank):
                dve.wait_ge(p_done[lane], i - lane)
                view = bank[:, 0:2 * PW].rearrange("p (s a x) -> p s x a", s=2, a=PARTS)[:, :, 0:GK, :]
                return nc.vector.tensor_reduce(pooled[:, 0, :, lane * GK:(lane + 1) * GK], view, AX.X, ALU.add)

            def sums_of_others(i):
                if active(i, 0):
                    dve.wait_ge(p_done[0], i)
                if active(i, 2):
                    ins = take_sums(i, 2, pb_ps)
                if active(i, 0):
                    ins = nc.vector.tensor_copy(pooled[:, 0, 0, 0:GK].rearrange("p (b k) -> p b k", k=K),
                                                first_out[:, 0:GROUP].unsqueeze(2).to_broadcast([P, GROUP, K]))
                if active(i, 2) or active(i, 0):
                    step(ins)
                    return split_sums(slice(0, LANES, 2))

            def sums_of_lane_1(i):
                step(take_sums(i, 1, pa_ps))
                return split_sums(slice(1, 2))

            def squares(i):
                dve.wait_ge(s_done, i)
                for u in range(2):
                    to = s_sb[:, :].rearrange("p (x u k) -> p u k x", u=2, k=2)[:, u, :, :]
                    ins = nc.vector.tensor_reduce(to, s_out[:, u, :, :, :].rearrange("p k a x -> p k x a"), AX.X, ALU.add)
                step(ins)
                tt(sq[:, :], s_sb[:, :], s_sb[:, :], ALU.mult).then_inc(sq_ready, 1)

            def factors(i):
                n2, n2p1, ta, tb, r, tc, td, f = (t[0:NORM_ROWS, :] for t in rs)
                dve.wait_ge(n_done, i)
                g = guess[0:NORM_ROWS, :]
                r0 = g.bitcast(F32)
                nc.vector.tensor_copy(n2, norm_out)
                step(nc.vector.tensor_scalar(g, norm_out.bitcast(I32), -0.5, RSQRT_MAGIC, ALU.mult, ALU.add))
                step(tt(ta, n2, r0, ALU.mult))
                step(nc.vector.scalar_tensor_tensor(tb, ta, -RSQRT_C0, r0, ALU.mult, ALU.mult))
                step(nc.vector.scalar_tensor_tensor(r, tb, RSQRT_C1, r0, ALU.add, ALU.mult))
                step(tt(ta, n2, r, ALU.mult))
                nc.vector.tensor_scalar(n2p1, n2, 1.0, None, ALU.add)
                step(tt(tb, ta, r, ALU.mult))
                step(nc.vector.scalar_tensor_tensor(tc, tb, -10.0 / 3, tb, ALU.add, ALU.mult))
                step(nc.vector.scalar_tensor_tensor(td, tc, 5.0, ta, ALU.add, ALU.mult))
                step(nc.vector.scalar_tensor_tensor(ta, td, 1e-12 * 8 / 3, n2p1, ALU.add, ALU.mult))
                step(nc.vector.reciprocal(tb, ta))
                step(nc.vector.scalar_tensor_tensor(f, n2, 8.0 / 3, tb, ALU.mult, ALU.mult))
                shape = [NORM_ROWS, 2, NORM_ROWS]
                tt(diag[0:NORM_ROWS, :, :], ident_f[0:NORM_ROWS, 0:NORM_ROWS].unsqueeze(1).to_broadcast(shape),
                   f.unsqueeze(2).to_broadcast(shape), ALU.mult).then_inc(diag_ready, 1)

            def capsules(i):
                dve.wait_ge(f_done, i)
                step(tt(v_sb[:, 0, :], s_sb[:, :], factor_out, ALU.mult))
                if active(i, 0) or active(i, 1):
                    two = 2 * GK
                    step(less_part(v_sb[:, 1, 0:two], v_sb[:, 0, 0:two]))
                    less_part(v_sb[:, 2, 0:two], v_sb[:, 1, 0:two]).then_inc(v_ready, 1)
                    tt(qb[:, 0, 1, :, 0:GK].rearrange("p l (b k) -> p l b k", k=K),
                       v_sb[:, 0, 0:two].rearrange("p (l b k) -> p l b k", l=2, k=K),
                       bias_sb[:, :].unsqueeze(1).unsqueeze(1).to_broadcast([P, 2, GROUP, K]), ALU.mult)
                if active(i, 2):
                    tt(att[:, :, :], v_sb[:, 0, 2 * GK:3 * GK].rearrange("p (b k) -> p b k", k=K),
                       last_t[:, :].unsqueeze(2).to_broadcast([P, GROUP, K]), ALU.mult).then_inc(prod_ready, 1)

            def take_back(i):
                dve.wait_ge(q_done, i)
                for u in range(2):
                    for lane in range(2):
                        to = qb[:, 0, 0, lane, 0:GK].rearrange("p (x u k) -> p u k x", u=2, k=2)[:, u, :, :]
                        view = q_out[:, u, :, :, lane * GROUP:(lane + 1) * GROUP].rearrange("p k a x -> p k x a")
                        ins = nc.vector.tensor_reduce(to, view, AX.X, ALU.add)
                step(ins)

            def back_parts(lane):
                q = [qb[:, a, :, lane, :] for a in range(PARTS)]
                step(less_part(q[1], q[0]))
                less_part(q[2], q[1]).then_inc(qb_ready[lane], 1)

            def attention_exponents(i):
                dve.wait_ge(a_done, i - 2)
                sums = att_out.rearrange("p (b k) -> p b k", k=K)
                step(nc.vector.tensor_reduce(att_top[:, :], sums, AX.X, ALU.max))
                tt(att_less[:, :, :], sums, att_top[:, :].unsqueeze(2).to_broadcast([P, GROUP, K]), ALU.subtract)\
                    .then_inc(att_less_ready, 1)

            def finish(i, part):
                if part == 0:
                    dve.wait_ge(att_exp_done, i - 2)
                    v3 = v_sb[:, 0, 2 * GK:3 * GK].rearrange("p (b k) -> p b k", k=K)
                    nc.vector.tensor_reduce(att_total[:, :], att_ex[:, :, :], AX.X, ALU.add)
                    note(tt(att[:, :, :], att_ex[:, :, :], v3, ALU.mult))
                elif part == 1:
                    after(steps[0])
                    nc.vector.reciprocal(att_top[:, :], att_total[:, :])
                    note(nc.vector.tensor_reduce(att_sum[:, :], att[:, :, :], AX.X, ALU.add))
                else:
                    after(steps[0])
                    tt(final_t[:, bass.ds((i - 3) * GROUP, GROUP)], att_sum[:, :], att_top[:, :], ALU.mult)\
                        .then_inc(final_done, 1)

            def take_logits(i, lane, u):
                dve.wait_ge(l_done[lane][u], i - lane)
                tiles = HALF if u == 0 else TILES - HALF
                ins = nc.vector.tensor_reduce(
                    summed[:, lane, HALF * u:HALF * u + tiles, :],
                    l_ps[:, u, 0:tiles * LW].rearrange("p (t a x) -> p t x a", t=tiles, a=PARTS), AX.X, ALU.add)
                if lane == 1:
                    ins.then_inc(l_read[u], 1)
                return ins

            def weights(i, b, lane):
                flat = "p t x -> p (t x)"
                of = slice(lane * PADT, (lane + 1) * PADT)
                x = logit[:, lane, :, :]
                step(tt(masked[:, lane, :, :].rearrange(flat), summed[:, lane, :, :].rearrange(flat),
                        mask[(b - 1 - lane) % BUFS][:, :, :].rearrange(flat), ALU.mult))
                step(tt(x, masked[:, lane, :, 0:K], masked[:, lane, :, K:SK], ALU.add))
                if lane == 1:
                    step(tt(x, x, before[:, :, :], ALU.add))
                step(nc.vector.tensor_reduce(top[:, of], x, AX.X, ALU.max))
                tt(less[:, of, :], x, top[:, of].unsqueeze(2).to_broadcast([P, PADT, K]), ALU.subtract)\
                    .then_inc(less_ready[lane], 1)
                if lane == 0:
                    nc.vector.tensor_copy(before[:, :, :], x)
                    if active(i, 1):
                        last_items(i, b)
                elif active(i, 2):
                    finish(i, 0)
                dve.wait_ge(exp_done[lane], i - lane)
                summed_up = note(nc.vector.tensor_reduce(total[:, of], ex[:, of, :], AX.X, ALU.add))
                if lane == 1 and active(i, 2):
                    finish(i, 1)
                after(summed_up)
                inverted = note(nc.vector.reciprocal(inv[:, of], total[:, of]))
                if lane == 1 and active(i, 2):
                    finish(i, 2)
                after(inverted)
                step(tt(share[:, of, :], ex[:, of, :], inv[:, of].unsqueeze(2).to_broadcast([P, PADT, K]), ALU.mult))
                step(tt(c_sb[:, lane, 0, :].rearrange("p (t s k) -> p t s k", s=SLOTS, k=K),
                        slot_sb[:, :, :].rearrange("p t (s k) -> p t s k", k=K),
                        share[:, of, :].unsqueeze(2).to_broadcast([P, PADT, SLOTS, K]), ALU.mult))
                step(less_part(c_sb[:, lane, 1, :], c_sb[:, lane, 0, :]))
                less_part(c_sb[:, lane, 2, :], c_sb[:, lane, 1, :]).then_inc(c_ready[lane], 1)

            def last_items(i, b):
                dve.wait_ge(et_copied, PARTS * CHUNKS * (i - 1))
                nc.vector.tensor_reduce(
                    last_t[:, :], emb_t[(b - 2) % BUFS][:, :, SEQ - 1:TILES * P:SEQ].rearrange("p a b -> p b a"),
                    AX.X, ALU.add).then_inc(last_read, 1)

            def body(i, b, use, count):
                base[0], steps[0] = count, 0
                has_front = not isinstance(i, int) or i < NG
                routed = active(i, 0) or active(i, 1)
                if has_front:
                    make_mask(i, b, use)
                if isinstance(i, int) and i == 0:
                    lows(i, b, 0)
                    for c in range(1, CHUNKS):
                        rests(i, b, c)
                        lows(i, b, c)
                    return steps[0]
                ins = sums_of_others(i)
                if has_front:
                    lows(i, b, 0)
                if active(i, 1):
                    ins = sums_of_lane_1(i)
                ins.then_inc(pooled_ready, 1)
                if has_front:
                    rests(i, b, 1)
                    lows(i, b, 1)
                squares(i)
                if has_front:
                    rests(i, b, 2)
                factors(i)
                if has_front:
                    lows(i, b, 2)
                capsules(i)
                if has_front:
                    rests(i, b, 3)
                if routed:
                    take_back(i)
                if active(i, 1):
                    back_parts(1)
                if active(i, 2):
                    attention_exponents(i)
                if active(i, 0):
                    back_parts(0)
                if has_front:
                    lows(i, b, 3)
                    rests(i, b, 4)
                if active(i, 1):
                    take_logits(i, 1, 0)
                if has_front:
                    lows(i, b, 4)
                if active(i, 1):
                    take_logits(i, 1, 1)
                    dve.wait_ge(l_read[1], i - 1)
                    weights(i, b, 1)
                elif active(i, 2):
                    for part in range(3):
                        finish(i, part)
                if active(i, 0):
                    for u in range(2):
                        ins = take_logits(i, 0, u)
                    step(ins)
                    weights(i, b, 0)
                elif active(i, 1):
                    last_items(i, b)
                return steps[0]

            done = steps[0]
            for i in range(BUFS):
                done += body(i, i, 0, done)
            for first, end in ((1, FIRST_SCORE // BUFS), (FIRST_SCORE // BUFS, NG // BUFS)):
                with dve.Fori(first, end) as j:
                    for b in range(BUFS):
                        n = body(BUFS * j + b, b, j, done - first * BUFS * BODY_STEPS + BODY_STEPS * (BUFS * j + b))
                        assert n == BODY_STEPS, n
                done += BODY_STEPS * BUFS * (end - first)
            for i in range(NG // BUFS * BUFS, LAST_BODY + 1):
                done += body(i, i % BUFS, i // BUFS, done)


BODY_STEPS = 42


def kernel(r_seq, L0_rec_emb_table, L0_rec_s_w, L0_rec_s_b):
    import concourse.bacc as bacc
    from concourse.bass_utils import run_bass_kernel_spmd

    r_seq, table, w, b = (np.asarray(x) for x in (r_seq, L0_rec_emb_table, L0_rec_s_w, L0_rec_s_b))
    position = np.arange(TILES * P).reshape(TILES, P).T
    slot = np.zeros((P, PADT, SLOTS, K), np.float32)
    for s in range(SLOTS):
        slot[:, :TILES, s, :] = (position // SEQ == np.array(FIRST_SEQ) + s)[:, :, None]
    arrays = {
        "index": np.ascontiguousarray(r_seq.reshape(NG, TILES, P).transpose(0, 2, 1)).view(np.uint32),
        "table": np.ascontiguousarray(table),
        "table_t": np.ascontiguousarray(table.T),
        "w": np.ascontiguousarray(w),
        "w_t": np.ascontiguousarray(w.reshape(HID, K, HID).transpose(2, 1, 0).reshape(HID, K * HID)),
        "bias": np.ascontiguousarray(b.reshape(K, HID).T),
        "bias_rows": np.ascontiguousarray(np.broadcast_to(b, (PARTS, K * HID))),
        "ident": np.eye(P, dtype=np.float32),
        "slot_mask": slot.reshape(P, -1),
    }
    nc = bacc.Bacc("TRN2", target_bir_lowering=False, num_devices=1)
    args = [nc.dram_tensor(n, a.shape, mybir.dt.from_np(a.dtype), kind="ExternalInput").ap() for n, a in arrays.items()]
    out = nc.dram_tensor("scores", (BATCH, ITEMS), F32, kind="ExternalOutput").ap()
    build(nc, *args, out)
    r = run_bass_kernel_spmd(nc, [arrays], core_ids=[0])
    return r.results[0]["scores"]
```
